# Optimizing a Trainium2 kernel written in Bass

```python
import numpy as np
import jax
import jax.numpy as jnp

def _softmax(x, axis=-1):
    return jax.nn.softmax(x, axis=axis)

def _gelu(x):
    return jax.nn.gelu(x, approximate=True)

def _silu(x):
    return jax.nn.silu(x)

def _sigmoid(x):
    return jax.nn.sigmoid(x)

def _layernorm(x, axis=-1, eps=1e-05):
    m = jnp.mean(x, axis=axis, keepdims=True)
    v = jnp.var(x, axis=axis, keepdims=True)
    return (x - m) / jnp.sqrt(v + eps)

def _scatter_add(tgt, idx, src, axis=0):
    return tgt.at[idx].add(src)

def _segment_sum(src, seg, n):
    return jax.ops.segment_sum(src, seg, n)
kernel_name = 'mk_decoder_postln_d1_seqx_r4_1eff5d'

def setup_inputs(seed: int=0):
    np.random.seed(seed)
    _w = jnp.asarray

    def _rec_inputs():
        import jax
        import jax.numpy as jnp
        _rk = jax.random.key(seed)
        x = 0.0002279 + 0.9999 * jax.random.normal(jax.random.fold_in(_rk, 1), (64, 256, 256), jnp.float32)
        _lenS = 256 - jax.random.randint(jax.random.fold_in(_rk, 7), (64,), 0, max(1, 256 // 4) + 1, jnp.int32)
        _lenS2 = 120 - jax.random.randint(jax.random.fold_in(_rk, 8), (64,), 0, max(1, 120 // 4) + 1, jnp.int32)
        _ctx_1024P = jax.random.normal(jax.random.fold_in(_rk, 11), (64, 16, 256), jnp.float32)
        _ctx_1024c = jax.random.dirichlet(jax.random.fold_in(_rk, 511), 0.3 * jnp.ones((16,), jnp.float32), (64, 120))
        _ctx_1024t = jnp.einsum('bsk,bkd->bsd', _ctx_1024c, _ctx_1024P)
        _ctx_1024t = _ctx_1024t * jax.lax.rsqrt(jnp.mean(jnp.square(_ctx_1024t)) + 1e-12) * 0.953939
        ctx_1024 = -0.000125008 + 0.999885 * (_ctx_1024t + 0.3 * jax.random.normal(jax.random.fold_in(_rk, 611), (64, 120, 256), jnp.float32))
        return (x, ctx_1024)
    x, ctx_1024 = _rec_inputs()

    def _L0_attn_setup():
        import jax, jax.numpy as jnp
        import numpy as np
        D_MODEL = 256
        D_STATE = 16
        D_CONV = 4
        EXPAND = 2
        HEADDIM = 64
        CHUNK = 64
        D_INNER = EXPAND * D_MODEL
        NHEADS = D_INNER // HEADDIM
        CONV_DIM = D_INNER + 2 * D_STATE
        D_IN_PROJ = 2 * D_INNER + 2 * D_STATE + NHEADS

        def silu(x):
            return x * jax.nn.sigmoid(x)

        def segsum(x):
            T = x.shape[-1]
            xe = jnp.repeat(x[..., None], T, axis=-1)
            mask_lower = jnp.tril(jnp.ones((T, T), bool), -1)
            xe = jnp.where(mask_lower, xe, 0.0)
            s = jnp.cumsum(xe, axis=-2)
            mask_diag = jnp.tril(jnp.ones((T, T), bool), 0)
            return jnp.where(mask_diag, s, -jnp.inf)

        def ssd(x, A, B, C, chunk):
            b, L, h, p = x.shape
            n = B.shape[-1]
            c = L // chunk
            x = x.reshape(b, c, chunk, h, p)
            A = A.reshape(b, c, chunk, h).transpose(0, 3, 1, 2)
            B = jnp.broadcast_to(B[:, :, None] if B.ndim == 3 else B, (b, L, h, n)).reshape(b, c, chunk, h, n)
            C = jnp.broadcast_to(C[:, :, None] if C.ndim == 3 else C, (b, L, h, n)).reshape(b, c, chunk, h, n)
            A_cumsum = jnp.cumsum(A, axis=-1)
            Lmat = jnp.exp(segsum(A))
            Y_diag = jnp.einsum('bclhn,bcshn,bhcls,bcshp->bclhp', C, B, Lmat, x)
            decay_states = jnp.exp(A_cumsum[:, :, :, -1:] - A_cumsum)
            states = jnp.einsum('bclhn,bhcl,bclhp->bchpn', B, decay_states, x)
            init = jnp.zeros_like(states[:, :1])
            states = jnp.concatenate([init, states], axis=1)
            A_last = jnp.pad(A_cumsum[:, :, :, -1], ((0, 0), (0, 0), (1, 0)))
            decay_chunk = jnp.exp(segsum(A_last))
            new_states = jnp.einsum('bhzc,bchpn->bzhpn', decay_chunk, states)
            states, final_state = (new_states[:, :-1], new_states[:, -1])
            state_decay_out = jnp.exp(A_cumsum)
            Y_off = jnp.einsum('bclhn,bchpn,bhcl->bclhp', C, states, state_decay_out)
            Y = (Y_diag + Y_off).reshape(b, L, h, p)
            return (Y, final_state)
        key = jax.random.key(seed)
        ks = jax.random.split(key, 8)
        B, L = (2, 1024)
        u = jax.random.normal(ks[0], (B, L, D_MODEL), dtype=jnp.float32)
        W_in = jax.random.normal(ks[1], (D_IN_PROJ, D_MODEL), dtype=jnp.float32) * 0.02
        conv_w = jax.random.normal(ks[2], (CONV_DIM, 1, D_CONV), dtype=jnp.float32) * 0.2
        conv_b = jnp.zeros((CONV_DIM,), dtype=jnp.float32)
        dt_bias = jax.random.uniform(ks[3], (NHEADS,), dtype=jnp.float32, minval=-4.0, maxval=1.0)
        A_log = jnp.full((NHEADS,), -np.log(2.0), dtype=jnp.float32)
        D = jnp.ones((NHEADS,), dtype=jnp.float32)
        norm_w = jnp.ones((D_INNER,), dtype=jnp.float32)
        W_out = jax.random.normal(ks[4], (D_MODEL, D_INNER), dtype=jnp.float32) * 0.02
        return {'u': u, 'W_in': W_in, 'conv_w': conv_w, 'conv_b': conv_b, 'dt_bias': dt_bias, 'A_log': A_log, 'D': D, 'norm_w': norm_w, 'W_out': W_out}
    _L0_attn_all = _L0_attn_setup()
    _L0_attn_in = {k: v for k, v in _L0_attn_all.items() if k in ('W_in', 'conv_w', 'conv_b', 'dt_bias', 'A_log', 'D', 'norm_w', 'W_out')}
    del _L0_attn_all

    def _L0_xattn_setup():
        import jax, jax.numpy as jnp
        import numpy as np
        DIM = 256
        HEADS = 8
        DIM_HEAD = 64
        INNER = HEADS * DIM_HEAD
        EPS = 1e-05

        def layernorm(x, w, b):
            mu = jnp.mean(x, axis=-1, keepdims=True)
            var = jnp.var(x, axis=-1, keepdims=True)
            return (x - mu) * jax.lax.rsqrt(var + EPS) * w + b
        key = jax.random.key(seed)
        ks = jax.random.split(key, 7)
        b, n_media, n_lat = (16, 512, 64)
        x = jax.random.normal(ks[0], (b, n_media, DIM), dtype=jnp.float32)
        latents = jax.random.normal(ks[1], (b, n_lat, DIM), dtype=jnp.float32)
        ln_m_w = jnp.ones((DIM,), jnp.float32)
        ln_m_b = jnp.zeros((DIM,), jnp.float32)
        ln_l_w = jnp.ones((DIM,), jnp.float32)
        ln_l_b = jnp.zeros((DIM,), jnp.float32)
        Wq = jax.random.normal(ks[2], (DIM, INNER), dtype=jnp.float32) * DIM ** (-0.5)
        Wkv = jax.random.normal(ks[3], (DIM, 2 * INNER), dtype=jnp.float32) * DIM ** (-0.5)
        Wout = jax.random.normal(ks[4], (INNER, DIM), dtype=jnp.float32) * INNER ** (-0.5)
        return {'x': x, 'latents': latents, 'ln_m_w': ln_m_w, 'ln_m_b': ln_m_b, 'ln_l_w': ln_l_w, 'ln_l_b': ln_l_b, 'Wq': Wq, 'Wkv': Wkv, 'Wout': Wout}
    _L0_xattn_all = _L0_xattn_setup()
    _L0_xattn_in = {k: v for k, v in _L0_xattn_all.items() if k in ('ln_m_w', 'ln_m_b', 'ln_l_w', 'ln_l_b', 'Wq', 'Wkv', 'Wout')}
    del _L0_xattn_all

    def _L0_ffn_setup():
        import jax, jax.numpy as jnp
        import numpy as np
        B, S, DIM = (4, 1024, 256)
        BASE_COUPLING = 0.1
        NUM_CYCLES = 3

        def _gelu(x):
            return jax.nn.gelu(x, approximate=False)

        def _coupling_net(h, w1, b1, w2, b2, w3, b3, w4, b4):
            h = _gelu(h @ w1 + b1)
            h = _gelu(h @ w2 + b2)
            h = _gelu(h @ w3 + b3)
            return jax.nn.sigmoid(h @ w4 + b4)

        def _global_net(h, w1, b1, w2, b2, w3, b3):
            h = _gelu(h @ w1 + b1)
            h = _gelu(h @ w2 + b2)
            return jax.nn.sigmoid(h @ w3 + b3)

        def _twist(x):
            o_r, o_i, p_r, p_i = jnp.split(x, 4, axis=-1)
            return jnp.concatenate([p_r, -p_i, -o_r, o_i], axis=-1)
        key = jax.random.key(seed)
        ks = jax.random.split(key, 9)
        d = DIM

        def w(k, fan_in, fan_out):
            return jax.random.normal(k, (fan_in, fan_out), dtype=jnp.float32) / np.sqrt(fan_in).astype(np.float32)
        inp = {'x': jax.random.normal(ks[0], (B, S, d), dtype=jnp.float32)}
        cn_dims = [(d, d), (d, d // 2), (d // 2, d // 4), (d // 4, 1)]
        for i, (a, b) in enumerate(cn_dims):
            inp[f'cn_w{i + 1}'] = w(ks[1 + i], a, b)
            inp[f'cn_b{i + 1}'] = jnp.zeros((b,), dtype=jnp.float32)
        gc_dims = [(d, d // 2), (d // 2, d // 4), (d // 4, 1)]
        for i, (a, b) in enumerate(gc_dims):
            inp[f'gc_w{i + 1}'] = w(ks[5 + i], a, b)
            inp[f'gc_b{i + 1}'] = jnp.zeros((b,), dtype=jnp.float32)
        inp['adaptive_range'] = jnp.full((1,), 0.2, dtype=jnp.float32)
        return inp
    _L0_ffn_all = _L0_ffn_setup()
    _L0_ffn_in = {k: v for k, v in _L0_ffn_all.items() if k in ('cn_w1', 'cn_b1', 'cn_w2', 'cn_b2', 'cn_w3', 'cn_b3', 'cn_w4', 'cn_b4', 'gc_w1', 'gc_b1', 'gc_w2', 'gc_b2', 'gc_w3', 'gc_b3', 'adaptive_range')}
    del _L0_ffn_all
    return {'x': x, 'ctx_1024': ctx_1024, 'L0_attn_W_in': _L0_attn_in['W_in'], 'L0_attn_conv_w': _L0_attn_in['conv_w'], 'L0_attn_conv_b': _L0_attn_in['conv_b'], 'L0_attn_dt_bias': _L0_attn_in['dt_bias'], 'L0_attn_A_log': _L0_attn_in['A_log'], 'L0_attn_D': _L0_attn_in['D'], 'L0_attn_norm_w': _L0_attn_in['norm_w'], 'L0_attn_W_out': _L0_attn_in['W_out'], 'L0_xattn_ln_m_w': _L0_xattn_in['ln_m_w'], 'L0_xattn_ln_m_b': _L0_xattn_in['ln_m_b'], 'L0_xattn_ln_l_w': _L0_xattn_in['ln_l_w'], 'L0_xattn_ln_l_b': _L0_xattn_in['ln_l_b'], 'L0_xattn_Wq': _L0_xattn_in['Wq'], 'L0_xattn_Wkv': _L0_xattn_in['Wkv'], 'L0_xattn_Wout': _L0_xattn_in['Wout'], 'L0_ffn_cn_w1': _L0_ffn_in['cn_w1'], 'L0_ffn_cn_b1': _L0_ffn_in['cn_b1'], 'L0_ffn_cn_w2': _L0_ffn_in['cn_w2'], 'L0_ffn_cn_b2': _L0_ffn_in['cn_b2'], 'L0_ffn_cn_w3': _L0_ffn_in['cn_w3'], 'L0_ffn_cn_b3': _L0_ffn_in['cn_b3'], 'L0_ffn_cn_w4': _L0_ffn_in['cn_w4'], 'L0_ffn_cn_b4': _L0_ffn_in['cn_b4'], 'L0_ffn_gc_w1': _L0_ffn_in['gc_w1'], 'L0_ffn_gc_b1': _L0_ffn_in['gc_b1'], 'L0_ffn_gc_w2': _L0_ffn_in['gc_w2'], 'L0_ffn_gc_b2': _L0_ffn_in['gc_b2'], 'L0_ffn_gc_w3': _L0_ffn_in['gc_w3'], 'L0_ffn_gc_b3': _L0_ffn_in['gc_b3'], 'L0_ffn_adaptive_range': _L0_ffn_in['adaptive_range']}

def reference(x, ctx_1024, L0_attn_W_in, L0_attn_conv_w, L0_attn_conv_b, L0_attn_dt_bias, L0_attn_A_log, L0_attn_D, L0_attn_norm_w, L0_attn_W_out, L0_xattn_ln_m_w, L0_xattn_ln_m_b, L0_xattn_ln_l_w, L0_xattn_ln_l_b, L0_xattn_Wq, L0_xattn_Wkv, L0_xattn_Wout, L0_ffn_cn_w1, L0_ffn_cn_b1, L0_ffn_cn_w2, L0_ffn_cn_b2, L0_ffn_cn_w3, L0_ffn_cn_b3, L0_ffn_cn_w4, L0_ffn_cn_b4, L0_ffn_gc_w1, L0_ffn_gc_b1, L0_ffn_gc_w2, L0_ffn_gc_b2, L0_ffn_gc_w3, L0_ffn_gc_b3, L0_ffn_adaptive_range):
    import jax
    import jax.numpy as jnp

    def _L0_attn_ref(u, W_in, conv_w, conv_b, dt_bias, A_log, D, norm_w, W_out):
        import jax, jax.numpy as jnp
        import numpy as np
        D_MODEL = 256
        D_STATE = 16
        D_CONV = 4
        EXPAND = 2
        HEADDIM = 64
        CHUNK = 64
        D_INNER = EXPAND * D_MODEL
        NHEADS = D_INNER // HEADDIM
        CONV_DIM = D_INNER + 2 * D_STATE
        D_IN_PROJ = 2 * D_INNER + 2 * D_STATE + NHEADS

        def silu(x):
            return x * jax.nn.sigmoid(x)

        def segsum(x):
            T = x.shape[-1]
            xe = jnp.repeat(x[..., None], T, axis=-1)
            mask_lower = jnp.tril(jnp.ones((T, T), bool), -1)
            xe = jnp.where(mask_lower, xe, 0.0)
            s = jnp.cumsum(xe, axis=-2)
            mask_diag = jnp.tril(jnp.ones((T, T), bool), 0)
            return jnp.where(mask_diag, s, -jnp.inf)

        def ssd(x, A, B, C, chunk):
            b, L, h, p = x.shape
            n = B.shape[-1]
            c = L // chunk
            x = x.reshape(b, c, chunk, h, p)
            A = A.reshape(b, c, chunk, h).transpose(0, 3, 1, 2)
            B = jnp.broadcast_to(B[:, :, None] if B.ndim == 3 else B, (b, L, h, n)).reshape(b, c, chunk, h, n)
            C = jnp.broadcast_to(C[:, :, None] if C.ndim == 3 else C, (b, L, h, n)).reshape(b, c, chunk, h, n)
            A_cumsum = jnp.cumsum(A, axis=-1)
            Lmat = jnp.exp(segsum(A))
            Y_diag = jnp.einsum('bclhn,bcshn,bhcls,bcshp->bclhp', C, B, Lmat, x)
            decay_states = jnp.exp(A_cumsum[:, :, :, -1:] - A_cumsum)
            states = jnp.einsum('bclhn,bhcl,bclhp->bchpn', B, decay_states, x)
            init = jnp.zeros_like(states[:, :1])
            states = jnp.concatenate([init, states], axis=1)
            A_last = jnp.pad(A_cumsum[:, :, :, -1], ((0, 0), (0, 0), (1, 0)))
            decay_chunk = jnp.exp(segsum(A_last))
            new_states = jnp.einsum('bhzc,bchpn->bzhpn', decay_chunk, states)
            states, final_state = (new_states[:, :-1], new_states[:, -1])
            state_decay_out = jnp.exp(A_cumsum)
            Y_off = jnp.einsum('bclhn,bchpn,bhcl->bclhp', C, states, state_decay_out)
            Y = (Y_diag + Y_off).reshape(b, L, h, p)
            return (Y, final_state)
        b, L, _ = u.shape
        A = -jnp.exp(A_log)
        zxbcdt = u @ W_in.T
        z = zxbcdt[..., :D_INNER]
        xBC = zxbcdt[..., D_INNER:D_INNER + CONV_DIM]
        dt = jax.nn.softplus(zxbcdt[..., -NHEADS:] + dt_bias)
        conv = jax.lax.conv_general_dilated(xBC.transpose(0, 2, 1), conv_w, window_strides=(1,), padding=[(D_CONV - 1, 0)], feature_group_count=CONV_DIM)
        xBC = silu((conv + conv_b[None, :, None]).transpose(0, 2, 1))
        x = xBC[..., :D_INNER].reshape(b, L, NHEADS, HEADDIM)
        Bm = xBC[..., D_INNER:D_INNER + D_STATE]
        Cm = xBC[..., D_INNER + D_STATE:]
        y, _ = ssd(x * dt[..., None], A * dt, Bm, Cm, CHUNK)
        y = y + x * D[:, None]
        y = y.reshape(b, L, D_INNER)
        y = y * silu(z)
        y = y * jax.lax.rsqrt(jnp.mean(y * y, axis=-1, keepdims=True) + 1e-05) * norm_w
        return y @ W_out.T

    def _L0_xattn_ref(x, latents, ln_m_w, ln_m_b, ln_l_w, ln_l_b, Wq, Wkv, Wout):
        import jax, jax.numpy as jnp
        import numpy as np
        DIM = 256
        HEADS = 8
        DIM_HEAD = 64
        INNER = HEADS * DIM_HEAD
        EPS = 1e-05

        def layernorm(x, w, b):
            mu = jnp.mean(x, axis=-1, keepdims=True)
            var = jnp.var(x, axis=-1, keepdims=True)
            return (x - mu) * jax.lax.rsqrt(var + EPS) * w + b
        scale = DIM_HEAD ** (-0.5)
        xn = layernorm(x, ln_m_w, ln_m_b)
        ln = layernorm(latents, ln_l_w, ln_l_b)
        b = xn.shape[0]
        q = ln @ Wq
        kv_input = jnp.concatenate([xn, ln], axis=-2)
        kv = kv_input @ Wkv
        k, v = jnp.split(kv, 2, axis=-1)

        def to_heads(t):
            return t.reshape(b, t.shape[1], HEADS, DIM_HEAD).transpose(0, 2, 1, 3)
        q, k, v = (to_heads(q) * scale, to_heads(k), to_heads(v))
        sim = jnp.einsum('bhid,bhjd->bhij', q, k)
        attn = jax.nn.softmax(sim, axis=-1)
        out = jnp.einsum('bhij,bhjd->bhid', attn, v)
        out = out.transpose(0, 2, 1, 3).reshape(b, out.shape[2], INNER)
        return out @ Wout

    def _L0_ffn_ref(x, cn_w1, cn_b1, cn_w2, cn_b2, cn_w3, cn_b3, cn_w4, cn_b4, gc_w1, gc_b1, gc_w2, gc_b2, gc_w3, gc_b3, adaptive_range):
        import jax, jax.numpy as jnp
        import numpy as np
        B, S, DIM = (4, 1024, 256)
        BASE_COUPLING = 0.1
        NUM_CYCLES = 3

        def _gelu(x):
            return jax.nn.gelu(x, approximate=False)

        def _coupling_net(h, w1, b1, w2, b2, w3, b3, w4, b4):
            h = _gelu(h @ w1 + b1)
            h = _gelu(h @ w2 + b2)
            h = _gelu(h @ w3 + b3)
            return jax.nn.sigmoid(h @ w4 + b4)

        def _global_net(h, w1, b1, w2, b2, w3, b3):
            h = _gelu(h @ w1 + b1)
            h = _gelu(h @ w2 + b2)
            return jax.nn.sigmoid(h @ w3 + b3)

        def _twist(x):
            o_r, o_i, p_r, p_i = jnp.split(x, 4, axis=-1)
            return jnp.concatenate([p_r, -p_i, -o_r, o_i], axis=-1)
        global_context = x.mean(axis=1, keepdims=True)
        gf = _global_net(global_context, gc_w1, gc_b1, gc_w2, gc_b2, gc_w3, gc_b3)
        out = x
        for _ in range(NUM_CYCLES):
            tf = _coupling_net(out, cn_w1, cn_b1, cn_w2, cn_b2, cn_w3, cn_b3, cn_w4, cn_b4)
            combined = 0.7 * gf + 0.3 * tf
            coupling = BASE_COUPLING + adaptive_range * (combined - 0.5) * 2.0
            out = out + coupling * _twist(out)
        return out
    x = _layernorm(x + _L0_attn_ref(x, L0_attn_W_in, L0_attn_conv_w, L0_attn_conv_b, L0_attn_dt_bias, L0_attn_A_log, L0_attn_D, L0_attn_norm_w, L0_attn_W_out), axis=-1)
    x = _layernorm(x + _L0_xattn_ref(ctx_1024, x, L0_xattn_ln_m_w, L0_xattn_ln_m_b, L0_xattn_ln_l_w, L0_xattn_ln_l_b, L0_xattn_Wq, L0_xattn_Wkv, L0_xattn_Wout), axis=-1)
    x = _layernorm(x + _L0_ffn_ref(x, L0_ffn_cn_w1, L0_ffn_cn_b1, L0_ffn_cn_w2, L0_ffn_cn_b2, L0_ffn_cn_w3, L0_ffn_cn_b3, L0_ffn_cn_w4, L0_ffn_cn_b4, L0_ffn_gc_w1, L0_ffn_gc_b1, L0_ffn_gc_w2, L0_ffn_gc_b2, L0_ffn_gc_w3, L0_ffn_gc_b3, L0_ffn_adaptive_range), axis=-1)
    return x

_drawn_inputs = setup_inputs


def setup_inputs(seed=0):
    import zlib

    import numpy as np

    out = dict(_drawn_inputs(seed))
    spreads = {'L0_attn_conv_b': (0.0, 0.1),
     'L0_attn_A_log': (-0.6931471824645996, 0.6),
     'L0_attn_D': (1.0, 0.2),
     'L0_attn_norm_w': (1.0, 0.2),
     'L0_xattn_ln_m_w': (1.0, 0.2),
     'L0_xattn_ln_m_b': (0.0, 0.1),
     'L0_xattn_ln_l_w': (1.0, 0.2),
     'L0_xattn_ln_l_b': (0.0, 0.1),
     'L0_ffn_cn_b1': (0.0, 2.0),
     'L0_ffn_cn_b2': (0.0, 2.0),
     'L0_ffn_cn_b3': (0.0, 2.0),
     'L0_ffn_gc_b1': (0.0, 0.8),
     'L0_ffn_gc_b2': (0.0, 0.8)}
    factors = {'L0_attn_dt_bias': 8.0,
     'L0_ffn_cn_w1': 7.581,
     'L0_ffn_cn_w2': 7.813,
     'L0_ffn_cn_w3': 6.388,
     'L0_ffn_cn_w4': 6.975,
     'L0_ffn_gc_w1': 8.0,
     'L0_ffn_gc_w2': 8.0,
     'L0_ffn_gc_w3': 5.757}
    for name, (base, spread) in spreads.items():
        noise = np.random.default_rng([zlib.crc32(name.encode()), seed]).standard_normal(out[name].shape)
        drawn = base * np.exp(spread * noise) if base else spread * noise
        out[name] = jnp.asarray(drawn.astype(out[name].dtype))
    for name, factor in factors.items():
        out[name] = (out[name] * factor).astype(out[name].dtype)
    return out
```

```python
from functools import partial


class Token:

    def __init__(self, sem, value):
        self.sem, self.value = sem, value


class Lane:

    def __init__(self, stage, engine, sem):
        self.stage, self.engine, self.sem, self.count = stage, engine, sem, 0

    def __call__(self, build, *args, after=(), signal=True, by=1, **kw):
        if signal:
            self.count += by
        self.stage.steps[-1][1].append((self.engine, [t for t in after if t], partial(build, *args, **kw),
                                        self.sem if signal else None, by))
        return Token(self.sem, self.count) if signal else None


class Stage:

    def __init__(self, sems):
        self.steps = []
        self.pe, self.act, self.dve, self.pool, self.sp = (
            Lane(self, e, s) for e, s in zip(("pe", "act", "dve", "pool", "sp"), sems))

    def step(self, cost):
        self.steps.append((cost, []))

    def take(self):
        steps, self.steps = self.steps, []
        return steps


class Bank:

    def __init__(self, ap):
        self.ap, self.freed = ap, []


class Ring:

    def __init__(self, banks):
        self.banks, self.n = banks, 0

    def next(self):
        self.n += 1
        return self.banks[(self.n - 1) % len(self.banks)]


def deal(stages):
    total = [max(1, sum(c for c, _ in s)) for s in stages]
    at, done, out = [0] * len(stages), [0.0] * len(stages), []
    while any(at[i] < len(s) for i, s in enumerate(stages)):
        i = min((i for i, s in enumerate(stages) if at[i] < len(s)),
                key=lambda i: (done[i] + 0.5 * stages[i][at[i]][0]) / total[i])
        cost, ops = stages[i][at[i]]
        out += ops
        done[i] += cost
        at[i] += 1
    return out


def param_columns():
    names = [("conv_w", 20), ("conv_b", 5), ("D", 4), ("norm_w", 4), ("ln_m_w", 2), ("ln_m_b", 2),
             ("ln_l_w", 2), ("ln_l_b", 2), ("cn_b1", 2), ("cn_b2", 1), ("cn_b3", 1), ("cn_b4", 1),
             ("gc_b1", 1), ("gc_b2", 1), ("gc_b3", 1), ("range", 1), ("dt_bias", 1), ("A_log", 1)]
    cols, at = {}, 0
    for n, k in names:
        cols[n] = (at, at + k)
        at += k
    return cols, at


ROW_B, ROW_DT, ROW_C, TAIL = 0, 32, 64, 80


def decoder_layer(nc, x, xT, ctx_in, par_in, w_in, w_out, wq, wkv, wo, cw1, cw2, cw3, cw4, gw1, gw2, gw3, out):
    from contextlib import ExitStack
    from concourse import mybir

    F32, F32R, BF16 = mybir.dt.float32, mybir.dt.float32r, mybir.dt.bfloat16
    ALU, ACT, AX = mybir.AluOpType, mybir.ActivationFunctionType, mybir.AxisListType

    NSEQ, L, D = x.shape
    J = ctx_in.shape[1]
    P = 128
    KT = D // P
    TT = L // P
    H, HD, NS = 8, 64, 16
    DI = H * HD
    CT = DI // P
    NK = J + L
    JT = [(0, J)] + [(J + P * t, P) for t in range(TT)]
    TRI = L + P
    EPS = 1e-5
    cols, NPAR = param_columns()
    assert TT == 2 and KT == 2 and TRI == 384

    es = ExitStack()
    with es:
        def sb(name, shape, dt=F32):
            return es.enter_context(nc.sbuf_tensor(name, shape, dt))

        def sem(name):
            return es.enter_context(nc.semaphore(name))

        par = sb("par", [P, NPAR])

        def prm(name, i=0, rows=slice(0, P)):
            a = cols[name][0] + i
            return par[rows, a:a + 1]

        WIN = 2 * DI + TAIL
        w_in_hi, w_in_lo = sb("w_in_hi", [P, KT, WIN], F32R), sb("w_in_lo", [P, KT, WIN], F32R)
        wq_hi, wq_lo = sb("wq_hi", [P, KT, DI], F32R), sb("wq_lo", [P, KT, DI], F32R)
        wkv_hi, wkv_lo = sb("wkv_hi", [P, KT, 2 * DI], F32R), sb("wkv_lo", [P, KT, 2 * DI], F32R)
        w_out_sb, wo_sb = sb("w_out_sb", [P, CT, D]), sb("wo_sb", [P, CT, D])
        cw1_sb, cw2_sb = sb("cw1_sb", [P, KT, D]), sb("cw2_sb", [P, KT, P])
        cw3_sb, cw4_sb = sb("cw3_sb", [P, HD]), sb("cw4_sb", [P, 1])
        cw4_row = sb("cw4_row", [P, P])
        gw1_sb, gw2_sb = sb("gw1_sb", [P, KT, P]), sb("gw2_sb", [P, HD])
        gw3_sb, gw3_row = sb("gw3_sb", [P, 1]), sb("gw3_row", [P, P])
        ident, ones = sb("ident", [P, P]), sb("ones", [P, L])
        causal = sb("causal", [P, TRI])
        pick = sb("pick", [P, H, P], BF16)
        a_neg = sb("a_neg", [P, 1])
        minus_half = sb("minus_half", [P, TT])
        half_b4, half_g3 = sb("half_b4", [P, 1]), sb("half_g3", [P, 1])
        sign = sb("sign", [P, 1])
        tf_gain, gf_gain, c_base = sb("tf_gain", [P, 1]), sb("gf_gain", [P, 1]), sb("c_base", [P, 1])

        xT_sb, x_sb = sb("xT_sb", [P, 2, KT, L]), sb("x_sb", [P, 2, TT, D])
        ctx_sb = sb("ctx_sb", [P, 2, D])
        out_sb = sb("out_sb", [P, 2, TT, D])

        x_hi, x_lo = sb("x_hi", [P, KT, L], F32R), sb("x_lo", [P, KT, L], F32R)
        u, th = sb("u", [P, CT + 1, L]), sb("th", [P, CT + 1, L])
        xc, gate = sb("xc", [P, CT, L]), sb("gate", [P, CT, L])
        Bz, Cz = sb("Bz", [P, L]), sb("Cz", [P, L])
        dt_a, dt_e = sb("dt_a", [P, L]), sb("dt_e", [P, L])
        dc = sb("dc", [P, L])
        c_rest = sb("c_rest", [P, L])
        c_mid, c_parts = sb("c_mid", [P, L], BF16), sb("c_parts", [P, L], BF16)
        ncum, dt_tok = sb("ncum", [P, TT, H]), sb("dt_tok", [P, TT, H])
        G = sb("G", [P, TRI])
        Lm = sb("Lm", [P, H, TRI])
        xdt = sb("xdt", [P, TT, DI])
        g = sb("g", [P, CT, L])
        yD, sq = u[:, 0:CT, :], th[:, 0:CT, :]
        ms, rms = sb("ms", [P, TT]), sb("rms", [P, TT])
        x1_pre, x1 = sb("x1_pre", [P, TT, D]), sb("x1", [P, 2, TT, D])

        ctx_n, x1_n = sb("ctx_n", [P, D]), sb("x1_n", [P, TT, D])
        kv, kv_hi, kv_lo = sb("kv", [P, KT, NK]), sb("kv_hi", [P, KT, NK], F32R), sb("kv_lo", [P, KT, NK], F32R)
        qT = sb("qT", [P, CT, L])
        kz = sb("kz", [P, H, NK])
        V = sb("V", [P, len(JT), DI])
        NP = 4
        prob, psum_row, prow_inv = sb("prob", [P, NP, NK]), sb("psum_row", [P, NP]), sb("prow_inv", [P, NP])
        nmax = sb("nmax", [P, NP])
        probT = sb("probT", [P, NP, len(JT), L])
        oT = sb("oT", [P, CT, L])
        x2 = sb("x2", [P, TT, D])
        x2T = sb("x2T", [P, 2, KT, L])
        x2sum = sb("x2sum", [P, 2, KT])

        f_cur = sb("f_cur", [P, 2, KT, L])
        h1, h2, h3 = sb("h1", [P, KT, L]), sb("h2", [P, L]), sb("h3", [P, L])
        t4, cpl, tw = sb("t4", [P, L]), sb("cpl", [P, L]), sb("tw", [P, KT, L])
        g1, g2, tg = sb("g1", [P, 1]), sb("g2", [P, 1]), sb("tg", [P, 1])
        f_sum = tw

        w_raw = Lm[:, :, :].rearrange("p h t -> p (h t)")[:, 0:KT * WIN].rearrange("p (k n) -> p k n", k=KT)
        wkv_raw = probT[:, :, :, :].rearrange("p a j t -> p (a j t)")[:, 0:KT * 2 * DI].rearrange("p (k n) -> p k n", k=KT)
        wq_raw = u[:, :, :].rearrange("p c t -> p (c t)")[:, 0:KT * DI].rearrange("p (k n) -> p k n", k=KT)

        stat = {n: (sb(f"st_{n}", [P, TT, 6]), sb(f"mv_{n}", [P, TT, 2]), sb(f"ve_{n}", [P, TT]),
                    sb(f"rs_{n}", [P, TT])) for n in ("mix", "ctx", "lat", "att", "ffn")}

        banks = [Bank(es.enter_context(nc.psum_tensor(f"bank{i}", [P, 512], F32))) for i in range(8)]
        ring_a, ring_b, ring_c = Ring(banks[0:2]), Ring(banks[2:5]), Ring(banks[5:8])

        def stage(name):
            return Stage([sem(f"{name}_{e}") for e in ("pe", "act", "dve", "pool", "sp")])

        S, M, X, F = stage("setup"), stage("mixer"), stage("attn"), stage("ffn")
        loads = Stage([None] * 5)
        s_par, s_w = sem("s_par"), sem("s_w")
        s_x, s_ctx, s_out = ([sem(f"{n}{i}") for i in range(2)] for n in ("s_x", "s_ctx", "s_out"))
        mm, tr = nc.tensor.matmul, nc.tensor.transpose
        act = nc.scalar.activation
        ts, tt, stt, cp = (nc.vector.tensor_scalar, nc.vector.tensor_tensor,
                           nc.vector.scalar_tensor_tensor, nc.vector.tensor_copy)
        pts, ptt = nc.gpsimd.tensor_scalar, nc.gpsimd.tensor_tensor

        T = {}

        def tok(name, s):
            return T.get((name, s))

        S.step(1)
        n_w = 0

        def load_w(dst, src):
            S.steps[-1][1].append(("sp", [], partial(nc.sync.dma_start, dst, src), s_w, 16))

        S.steps[-1][1].append(("sp", [], partial(nc.sync.dma_start, par[:, :], par_in[:, :]), s_par, 16))
        par_in_tok = Token(s_par, 16)

        def load_seq(s):
            i, k = s % 2, s // 2 + 1
            ops = loads.steps[-1][1]
            ops.append(("sp", [t for t in (tok("xT_used", s - 2),) if t],
                        partial(nc.sync.dma_start, xT_sb[:, i, :, :], xT[s].rearrange("(k p) t -> p k t", p=P)), s_x[i], 16))
            ops.append(("sp", [t for t in (tok("x_used", s - 2),) if t],
                        partial(nc.sync.dma_start, x_sb[:, i, :, :], x[s].rearrange("(k p) d -> p k d", p=P)), s_x[i], 16))
            T["x_in", s] = Token(s_x[i], 32 * k)

        def load_ctx(s):
            i, k = s % 2, s // 2 + 1
            loads.steps[-1][1].append(("sp", [t for t in (tok("ctx_used", s - 2),) if t],
                                       partial(nc.sync.dma_start, ctx_sb[0:J, i, :], ctx_in[s]), s_ctx[i], 16))
            T["ctx_in", s] = Token(s_ctx[i], 16 * k)

        loads.step(1)
        load_w(w_raw[:, :, :], w_in.rearrange("(k p) n -> p k n", p=P))
        first_loads = loads
        load_seq(0)
        S.steps[-1][1].extend(first_loads.take()[0][1])
        for dst, src in ((wq_raw[:, :, :], wq.rearrange("(k p) n -> p k n", p=P)),
                         (wkv_raw[:, :, :], wkv.rearrange("(k p) n -> p k n", p=P)),
                         (w_out_sb[:, :, :], w_out.rearrange("(k p) n -> p k n", p=P)),
                         (wo_sb[:, :, :], wo.rearrange("(k p) n -> p k n", p=P)),
                         (cw1_sb[:, :, :], cw1.rearrange("(k p) n -> p k n", p=P)),
                         (cw2_sb[:, :, :], cw2.rearrange("(k p) n -> p k n", p=P)),
                         (cw3_sb[:, :], cw3), (cw4_sb[0:HD, :], cw4),
                         (gw1_sb[:, :, :], gw1.rearrange("(k p) n -> p k n", p=P)),
                         (gw2_sb[:, :], gw2), (gw3_sb[0:HD, :], gw3)):
            load_w(dst, src)
            n_w += 1
        w_tok = Token(s_w, 16 * (n_w + 1))

        pd, dv = S.pool, S.dve
        z_id = pd(nc.gpsimd.memset, ident[:, :], 0.0)
        z_ca = pd(nc.gpsimd.memset, causal[:, :], 1.0)
        z_pk = pd(nc.gpsimd.memset, pick[:, :, :], 0.0)
        id_ok = pd(nc.gpsimd.affine_select, out=ident[:, :], in_=ident[:, :], compare_op=ALU.not_equal, fill=1.0,
                   base=0, pattern=[[-1, P]], channel_multiplier=1, after=[z_id])
        for c0 in (0, L):
            z_ca = pd(nc.gpsimd.affine_select, out=causal[:, c0:c0 + P], in_=causal[:, c0:c0 + P],
                      compare_op=ALU.is_ge, fill=0.0, base=0, pattern=[[1, P]], channel_multiplier=-1, after=[z_ca])
        for r0 in (0, 32, 64):
            z_pk = pd(nc.gpsimd.affine_select, out=pick[:, :, :], in_=pick[:, :, :], compare_op=ALU.not_equal,
                      fill=1.0, base=-r0, pattern=[[-1, H], [0, P]], channel_multiplier=1, after=[z_pk])
        consts = [id_ok, z_ca, z_pk]
        dv(nc.vector.memset, ones[:, :], 1.0)
        for b in (Bz, Cz, dc, h3, gw3_row, cw4_row):
            dv(nc.vector.memset, b[:, :], 0.0)
        dv(nc.vector.memset, c_parts[:, :], 0.0)
        dv(nc.vector.memset, kz[:, :, :], 0.0)
        dv(nc.vector.memset, g2[:, :], 0.0)
        dv(nc.vector.memset, minus_half[:, :], -0.5)
        dv(nc.vector.memset, sign[0:64, :], 1.0)
        dv(nc.vector.memset, sign[64:P, :], -1.0)
        for b in banks:
            zeros = dv(nc.vector.memset, b.ap[:, :], 0.0)
        a0, a1 = cols["conv_w"][0], cols["conv_b"][1]
        dv(ts, par[:, a0:a1], par[:, a0:a1], 0.5, None, ALU.mult, after=[par_in_tok])
        dv(ts, half_b4[:, :], prm("cn_b4"), 0.5, None, ALU.mult)
        dv(ts, half_g3[:, :], prm("gc_b3"), 0.5, None, ALU.mult)
        dv(ts, tf_gain[:, :], prm("range"), sign[:, :], 0.3, ALU.mult, ALU.mult, after=[zeros])
        dv(ts, gf_gain[:, :], prm("range"), sign[:, :], 0.7, ALU.mult, ALU.mult)
        pars = dv(ts, c_base[:, :], sign[:, :], 0.1, None, ALU.mult)
        ea = S.act(act, a_neg[ROW_DT:ROW_DT + H, :], prm("A_log", 0, slice(ROW_DT, ROW_DT + H)), ACT.Exp, after=[par_in_tok])
        pars2 = dv(ts, a_neg[ROW_DT:ROW_DT + H, :], a_neg[ROW_DT:ROW_DT + H, :], -1.0, None, ALU.mult, after=[ea])
        win = dv(ts, w_raw[:, :, DI:2 * DI], w_raw[:, :, DI:2 * DI], 0.5, None, ALU.mult, after=[w_tok])
        wqs = dv(ts, wq_raw[:, :, :], wq_raw[:, :, :], float(HD) ** -0.5, None, ALU.mult)
        for raw, hi, lo, t in ((w_raw, w_in_hi, w_in_lo, win), (wq_raw, wq_hi, wq_lo, wqs), (wkv_raw, wkv_hi, wkv_lo, None)):
            for k in range(KT):
                t = dv(cp, hi[:, k, :], raw[:, k, :], after=[t])
                w_split = dv(tt, lo[:, k, :], raw[:, k, :], hi[:, k, :].bitcast(F32), ALU.subtract, after=[t])
        for k in range(CT):
            dv(ts, w_out_sb[:, k, :], w_out_sb[:, k, :], prm("norm_w", k), None, ALU.mult)
        dv(ts, cw4_row[0:HD, :], ones[0:HD, 0:P], cw4_sb[0:HD, :], None, ALU.mult)
        w_ready = dv(ts, gw3_row[0:HD, :], ones[0:HD, 0:P], gw3_sb[0:HD, :], None, ALU.mult)
        ready = [w_ready] + consts
        T["setup"] = ready

        def norm_stats(st, name, src, rows, ntile, after):
            stats, mv, ve, rs = stat[name]
            for i in range(ntile):
                t = st.dve(nc.vector.bn_stats, stats[0:rows, i, :], src[i], after=after)
            for i in range(ntile):
                t = st.dve(nc.vector.bn_aggr, mv[0:rows, i, :], stats[0:rows, i, :], after=[t])
            t = st.pool(pts, ve[0:rows, 0:ntile], mv[0:rows, 0:ntile, 1], EPS, None, ALU.add, after=[t])
            t = st.pool(ptt, rs[0:rows, 0:ntile], ve[0:rows, 0:ntile], minus_half[0:rows, 0:ntile], ALU.pow, after=[t])
            return t, [mv[0:rows, i, 0:1] for i in range(ntile)], [rs[0:rows, i:i + 1] for i in range(ntile)]

        def product3(st, dst, w_hi, w_lo, x_hi_, x_lo_, after, x_is_rhs=True):
            n = 0
            for k in range(KT):
                for w_, x_ in ((w_hi[k], x_hi_[k]), (w_lo[k], x_hi_[k]), (w_hi[k], x_lo_[k])):
                    a, b = (w_, x_) if x_is_rhs else (x_, w_)
                    n += 1
                    t = st.pe(mm, dst, a, b, start=n == 1, stop=n == 3 * KT, signal=n == 3 * KT,
                              after=after if n == 1 else ())
            return t

        def mixer_front(s):
            i = s % 2
            M.step(100)
            hi_ok = M.act(act, x_hi[:, :, :], xT_sb[:, i, :, :], ACT.Copy,
                          after=[tok("x_in", s), tok("in_proj", s - 1)])
            lo_ok = M.dve(tt, x_lo[:, :, :], xT_sb[:, i, :, :], x_hi[:, :, :].bitcast(F32), ALU.subtract, after=[hi_ok])
            T["xT_used", s] = lo_ok

            def project(dst, c0, n, after):
                return product3(M, dst, [w_in_hi[:, k, c0:c0 + n] for k in range(KT)],
                                [w_in_lo[:, k, c0:c0 + n] for k in range(KT)],
                                [x_hi[:, k, :] for k in range(KT)], [x_lo[:, k, :] for k in range(KT)], after)

            def conv(src, c, rows, ready_):
                t = M.act(act, u[0:rows, c, :], src, ACT.Identity, scale=prm("conv_w", 4 * c + 3, slice(0, rows)),
                          bias=prm("conv_b", c, slice(0, rows)), after=[ready_, tok("conv", s - 1), tok("g", s - 1)])
                return t

            def taps(src, c, rows, after):
                for d in (1, 2, 3):
                    after = [M.dve(stt, u[0:rows, c, d:L], src[:, 0:L - d], prm("conv_w", 4 * c + 3 - d, slice(0, rows)),
                                   u[0:rows, c, d:L], ALU.mult, ALU.add, after=after)]
                return after[0]

            M.step(650)
            b = ring_a.next()
            p_ok = project(b.ap[0:TAIL, 0:L], 2 * DI, TAIL, b.freed + T["setup"] + [hi_ok, lo_ok])
            c_ok = conv(b.ap[0:TAIL, 0:L], CT, TAIL, p_ok)
            u_ok = taps(b.ap[0:TAIL, 0:L], CT, TAIL, [c_ok])
            a_ok = M.dve(ts, dt_a[ROW_DT:ROW_DT + H, :], b.ap[ROW_DT:ROW_DT + H, 0:L],
                         prm("dt_bias", 0, slice(ROW_DT, ROW_DT + H)), None, ALU.add,
                         after=[p_ok, tok("dt", s - 1)])
            T["dt_a", s] = a_ok
            b.freed = [a_ok]
            t_ok = M.act(act, th[0:TAIL, CT, :], u[0:TAIL, CT, :], ACT.Tanh, after=[u_ok, tok("BC", s - 1)])
            M.dve(stt, Bz[0:NS, :], th[0:NS, CT, :], 1.0, u[0:NS, CT, :], ALU.add, ALU.mult,
                  after=[t_ok, tok("CB", s - 1)])
            T["BC", s] = M.dve(stt, Cz[0:NS, :], th[ROW_C:ROW_C + NS, CT, :], 1.0, u[ROW_C:ROW_C + NS, CT, :],
                               ALU.add, ALU.mult)

            for j in range(CT // 2):
                M.step(1300)
                b = ring_a.next()
                aps = [b.ap[:, 0:L], b.ap[:, L:2 * L]]
                after = b.freed + [hi_ok, lo_ok]
                for e in range(2):
                    p_ok = project(aps[e], (2 * j + e) * P, P, after)
                    after = []
                c_ok = [conv(aps[e], 2 * j + e, P, p_ok) for e in range(2)]
                u_ok = [taps(aps[e], 2 * j + e, P, c_ok) for e in range(2)]
                b.freed = [u_ok[1]]
                t_ok = M.act(act, th[:, 2 * j:2 * j + 2, :], u[:, 2 * j:2 * j + 2, :], ACT.Tanh, after=u_ok + [tok("ms", s - 1)])
                T["xc", s] = M.dve(stt, xc[:, 2 * j:2 * j + 2, :], th[:, 2 * j:2 * j + 2, :], 1.0,
                                   u[:, 2 * j:2 * j + 2, :], ALU.add, ALU.mult, after=[t_ok, tok("xc_used", s - 1)])
            T["conv", s] = T["xc", s]
            for j in range(CT // 2):
                M.step(1300)
                b = ring_a.next()
                after = b.freed
                for e in range(2):
                    p_ok = project(b.ap[:, e * L:(e + 1) * L], DI + (2 * j + e) * P, P, after)
                    after = []
                flat = b.ap[:, :].rearrange("p (e t) -> p e t", e=2)
                t_ok = M.act(act, th[:, 2 * j:2 * j + 2, :], flat, ACT.Tanh, after=[p_ok, T["xc", s]])
                g_ok = M.dve(stt, gate[:, 2 * j:2 * j + 2, :], th[:, 2 * j:2 * j + 2, :], 1.0, flat, ALU.add, ALU.mult,
                             after=[t_ok, tok("gate_used", s - 1)])
                b.freed = [g_ok]
            T["gate", s] = g_ok
            T["in_proj", s] = p_ok

        def mixer_dt(s):
            r = slice(ROW_DT, ROW_DT + H)
            M.step(1)
            n_ok = M.dve(stt, dt_e[r, :], dt_a[r, :], -1.0, dt_a[r, :], ALU.mult, ALU.min, after=[T["dt_a", s]])
            e_ok = M.act(act, dt_e[r, :], dt_e[r, :], ACT.Exp, after=[n_ok])
            l_ok = M.act(act, dt_e[r, :], dt_e[r, :], ACT.Ln, bias=ones[r, 0:1], after=[e_ok])
            d_ok = M.dve(stt, dc[r, :], dt_a[r, :], 0.0, dt_e[r, :], ALU.max, ALU.add,
                         after=[l_ok, tok("dc_used", s - 1)])
            T["dt", s] = d_ok
            a_ok = M.dve(ts, dt_e[r, :], dc[r, :], a_neg[r, :], None, ALU.mult, after=[d_ok])
            c_ok = M.dve(nc.vector.tensor_tensor_scan, dc[0:H, :], ones[r, :], dt_e[r, :], 0.0, ALU.mult, ALU.add,
                         after=[a_ok])
            t = M.pool(pts, c_parts[0:H, :], dc[0:H, :], 1.0, None, ALU.mult, after=[c_ok, tok("parts_used", s - 1)])
            t = M.pool(ptt, c_rest[0:H, :], dc[0:H, :], c_parts[0:H, :], ALU.subtract, after=[t])
            t = M.pool(pts, c_mid[0:H, :], c_rest[0:H, :], 1.0, None, ALU.mult, after=[t])
            M.dve(cp, c_parts[32:32 + H, :], c_rest[0:H, :], after=[t])
            T["parts", s] = M.dve(tt, c_parts[64:64 + H, :], c_rest[0:H, :], c_mid[0:H, :], ALU.subtract)
            T["cum", s] = c_ok

        def mixer_back(s):
            M.step(430)
            b = ring_c.next()
            for i in range(TT):
                t = M.pe(tr, b.ap[:, i * 64:i * 64 + 40], dc[0:40, i * P:(i + 1) * P], ident[0:40, 0:40],
                         after=b.freed + [T["cum", s]])
            T["dc_used", s] = t
            bt = b.ap[:, 0:64 * TT].rearrange("p (i c) -> p i c", i=TT)
            n_ok = M.dve(ts, ncum[:, :, :], bt[:, :, 0:H], -1.0, None, ALU.mult, after=[t, tok("decay", s - 1)])
            d_ok = M.dve(cp, dt_tok[:, :, :], bt[:, :, 32:32 + H])
            b.freed = [d_ok]

            M.step(650)
            b = ring_c.next()
            M.pe(mm, b.ap[:, 0:L], Bz[:, 0:P], Cz[:, :], start=True, stop=True, after=b.freed + [T["BC", s]], signal=False)
            t = M.pe(mm, b.ap[:, L:TRI], Bz[:, P:L], Cz[:, P:L], start=True, stop=True)
            T["CB", s] = t
            G_ok = M.dve(tt, G[:, :], b.ap[:, 0:TRI], causal[:, :], ALU.mult, after=[t])
            b.freed = [G_ok]

            for i in range(TT):
                M.step(440)
                b = ring_c.next()
                for c in range(CT):
                    t = M.pe(tr, b.ap[:, c * P:(c + 1) * P], xc[:, c, i * P:(i + 1) * P], ident[:, :], signal=c == CT - 1,
                             after=b.freed + [T["xc", s]] if c == 0 else ())
                xdt_ok = M.dve(tt, xdt[:, i, :].rearrange("p (h d) -> p h d", h=H), b.ap[:, :].rearrange("p (h d) -> p h d", h=H),
                               dt_tok[:, i, :].unsqueeze(2).broadcast_to([P, H, HD]), ALU.mult,
                               after=[t, d_ok, tok("y", s - 1)])
                b.freed = [xdt_ok]

            def decay(q):
                b = ring_c.next()
                for e in range(2):
                    t = M.pe(mm, b.ap[:, e * L:(e + 1) * L], pick[:, 2 * q + e, :], c_parts[:, :], start=True, stop=True,
                             signal=e == 1, after=b.freed + [T["parts", s]] if e == 0 else ())
                T["parts_used", s] = t
                for e in range(2):
                    h = 2 * q + e
                    for i, c0, c1, m0 in ((0, 0, L, 0), (1, P, L, L)):
                        x_ok = M.dve(ts, Lm[:, h, m0:m0 + c1 - c0], b.ap[:, e * L + c0:e * L + c1], ncum[:, i, h:h + 1],
                                     0.0, ALU.add, ALU.min, after=[t, n_ok, tok("y", s - 1)])
                b.freed = [x_ok]
                T["decay", s] = x_ok
                pair = Lm[:, 2 * q:2 * q + 2, :]
                e_ok = M.act(act, pair, pair, ACT.Exp, after=[x_ok])
                return M.pool(ptt, pair, pair, G[:, :].unsqueeze(1).broadcast_to([P, 2, TRI]), ALU.mult, after=[e_ok, G_ok])

            def y_pair(q, lm_ok):
                b = ring_c.next()
                for i, (c0, c1, m0) in enumerate(((0, L, 0), (P, L, L))):
                    for e in range(2):
                        h = 2 * q + e
                        t = M.pe(mm, b.ap[e * HD:(e + 1) * HD, c0:c1], xdt[:, i, h * HD:(h + 1) * HD],
                                 Lm[:, h, m0:m0 + c1 - c0], start=i == 0, stop=i == 1, signal=i == 1 and e == 1,
                                 after=b.freed + [lm_ok, xdt_ok] if i == 0 and e == 0 else ())
                T["y", s] = t
                y_ok = M.dve(stt, yD[:, q, :], xc[:, q, :], prm("D", q), b.ap[:, 0:L], ALU.mult, ALU.add,
                             after=[t])
                b.freed = [y_ok]
                T["xc_used", s] = y_ok
                g_ok = M.pool(ptt, g[:, q, :], yD[:, q, :], gate[:, q, :], ALU.mult,
                              after=[y_ok, tok("gate", s), tok("out_proj", s - 1)])
                T["gate_used", s] = T["g", s] = g_ok
                return g_ok, M.act(act, sq[:, q, :], g[:, q, :], ACT.Square, after=[g_ok, tok("gate", s)])

            ok = None
            for q in range(CT + 1):
                M.step(950)
                if q < CT:
                    nxt = decay(q)
                if q > 0:
                    g_ok, sq_ok = y_pair(q - 1, ok)
                ok = nxt

            M.step(850)
            t = M.pool(ptt, sq[:, 0:2, :], sq[:, 0:2, :], sq[:, 2:4, :], ALU.add, after=[sq_ok])
            t = M.pool(ptt, sq[:, 0, :], sq[:, 0, :], sq[:, 1, :], ALU.add, after=[t])
            b2 = ring_c.next()
            for i in range(TT):
                for c in range(CT):
                    o_ok = M.pe(mm, b2.ap[:, i * D:(i + 1) * D], g[:, c, i * P:(i + 1) * P], w_out_sb[:, c, :],
                                start=c == 0, stop=c == CT - 1, signal=c == CT - 1,
                                after=b2.freed + [g_ok] if i == 0 and c == 0 else ())
            T["out_proj", s] = o_ok
            M.step(3450)
            b = ring_c.next()
            for i in range(TT):
                m_ok = M.pe(mm, b.ap[:, 2 * i:2 * i + 2], sq[:, 0, i * P:(i + 1) * P], ones[:, 0:2], start=True, stop=True,
                            after=b.freed + [t])
            v_ok = M.dve(ts, ms[:, :], b.ap[:, 0:2 * TT].rearrange("p (i c) -> p i c", c=2)[:, :, 0], 1.0 / DI, EPS,
                         ALU.mult, ALU.add, after=[m_ok, tok("rms", s - 1)])
            b.freed = [v_ok]
            T["ms", s] = m_ok
            r_ok = M.pool(ptt, rms[:, :], ms[:, :], minus_half[:, :], ALU.pow, after=[v_ok, tok("x_used", s - 1)])
            T["rms", s] = r_ok
            for i in range(TT):
                t = M.dve(stt, x1_pre[:, i, :], b2.ap[:, i * D:(i + 1) * D], rms[:, i:i + 1], x_sb[:, s % 2, i, :],
                          ALU.mult, ALU.add, after=[r_ok, o_ok])
            b2.freed = [t]
            T["x_used", s] = t
            n_t, mean, rstd = norm_stats(M, "mix", [x1_pre[:, i, :] for i in range(TT)], P, TT, [t])
            for i in range(TT):
                t = M.dve(ts, x1[:, s % 2, i, :], x1_pre[:, i, :], mean[i], rstd[i], ALU.subtract, ALU.mult,
                          after=[n_t, tok("x1_used", s - 2)])
            T["x1", s] = t

        def attn_front(s):
            i2 = s % 2
            X.step(220)
            n_t, mean, rstd = norm_stats(X, "ctx", [ctx_sb[0:J, i2, :]], J, 1, [tok("ctx_in", s)])
            t = X.dve(ts, ctx_n[0:J, :], ctx_sb[0:J, i2, :], mean[0], rstd[0], ALU.subtract, ALU.mult,
                      after=[n_t, tok("ctxT", s - 1)])
            T["ctx_used", s] = t
            b = ring_b.next()
            for k in range(KT):
                c_ok = X.pe(tr, b.ap[:, k * J:(k + 1) * J], ctx_n[0:J, k * P:(k + 1) * P], ident[0:J, 0:J],
                            after=b.freed + [t] + T["setup"])
            T["ctxT", s] = c_ok
            for k in range(KT):
                kv_c = X.act(act, kv[:, k, 0:J], b.ap[:, k * J:(k + 1) * J], ACT.Identity, scale=prm("ln_m_w", k),
                             bias=prm("ln_m_b", k), after=[c_ok, tok("kv_used", s - 1)])
            b.freed = [kv_c]
            X.step(440)
            n_t, mean, rstd = norm_stats(X, "lat", [x1[:, i2, i, :] for i in range(TT)], P, TT, [T["x1", s]])
            for i in range(TT):
                t = X.dve(ts, x1_n[:, i, :], x1[:, i2, i, :], mean[i], rstd[i], ALU.subtract, ALU.mult,
                          after=[n_t, tok("x1T", s - 1)])
            b = ring_b.next()
            for k in range(KT):
                for i in range(TT):
                    l_ok = X.pe(tr, b.ap[:, k * L + i * P:k * L + (i + 1) * P], x1_n[:, i, k * P:(k + 1) * P], ident[:, :],
                                after=b.freed + [t])
            T["x1T", s] = l_ok
            for k in range(KT):
                kv_l = X.act(act, kv[:, k, J:NK], b.ap[:, k * L:(k + 1) * L], ACT.Identity, scale=prm("ln_l_w", k),
                             bias=prm("ln_l_b", k), after=[l_ok])
            b.freed = [kv_l]
            hi_ok = X.dve(cp, kv_hi[:, :, :], kv[:, :, :], after=[kv_l, kv_c, tok("proj", s - 1)])
            lo_ok = X.dve(tt, kv_lo[:, :, :], kv[:, :, :], kv_hi[:, :, :].bitcast(F32), ALU.subtract, after=[hi_ok])
            T["kv_used", s] = lo_ok
            x_ok = [hi_ok, lo_ok]

            def q_pair(j):
                b = ring_b.next()
                after = b.freed + x_ok
                for e in range(2):
                    c0 = (2 * j + e) * P
                    p_ok = product3(X, b.ap[:, e * L:(e + 1) * L], [wq_hi[:, k, c0:c0 + P] for k in range(KT)],
                                    [wq_lo[:, k, c0:c0 + P] for k in range(KT)], [kv_hi[:, k, J:NK] for k in range(KT)],
                                    [kv_lo[:, k, J:NK] for k in range(KT)], after)
                    after = []
                t = X.act(act, qT[:, 2 * j:2 * j + 2, :], b.ap[:, :].rearrange("p (e t) -> p e t", e=2), ACT.Copy,
                          after=[p_ok, tok("scores", s - 1)])
                b.freed = [t]
                T["qT", s] = t

            def k_tile(c):
                b = ring_b.next()
                p_ok = product3(X, b.ap[:, 0:NK], [wkv_hi[:, k, c * P:(c + 1) * P] for k in range(KT)],
                                [wkv_lo[:, k, c * P:(c + 1) * P] for k in range(KT)], [kv_hi[:, k, :] for k in range(KT)],
                                [kv_lo[:, k, :] for k in range(KT)], b.freed + x_ok)
                t1 = X.act(act, kz[0:HD, 2 * c, :], b.ap[0:HD, 0:NK], ACT.Copy, after=[p_ok, tok("scores", s - 1)])
                t2 = X.dve(cp, kz[HD:P, 2 * c + 1, :], b.ap[HD:P, 0:NK], after=[p_ok, tok("scores", s - 1)])
                b.freed = [t1, t2]
                T["kz", s] = [t1, t2]

            def v_tile(j):
                j0, n = JT[j]
                b = ring_b.next()
                p_ok = product3(X, b.ap[0:n, :], [wkv_hi[:, k, DI:2 * DI] for k in range(KT)],
                                [wkv_lo[:, k, DI:2 * DI] for k in range(KT)], [kv_hi[:, k, j0:j0 + n] for k in range(KT)],
                                [kv_lo[:, k, j0:j0 + n] for k in range(KT)], b.freed + x_ok, x_is_rhs=False)
                t = X.act(act, V[0:n, j, :], b.ap[0:n, :], ACT.Copy, after=[p_ok, tok("attn", s - 1)])
                b.freed = [t]
                T["V", s] = t
                T["proj", s] = p_ok

            for j in range(CT // 2):
                X.step(1300)
                q_pair(j)
            for c in range(CT):
                X.step(960)
                k_tile(c)
            for j in range(len(JT)):
                X.step(1300)
                v_tile(j)

        def attn_back(s):
            NU, LAG = H * TT, 2
            p_ok, pt_ok, o_ok = {}, {}, None

            def scores(n):
                h, i, r = n // TT, n % TT, n % NP
                b = ring_a.next()
                t = X.pe(mm, b.ap[:, 0:NK], qT[:, h // 2, i * P:(i + 1) * P], kz[:, h, :], start=True, stop=True,
                         after=b.freed + [T["qT", s]] + T["kz", s])
                T["scores", s] = t
                m_ok = X.dve(nc.vector.tensor_reduce, nmax[:, r:r + 1], b.ap[:, 0:NK], AX.X, ALU.max, negate=True,
                             after=[t, T.get("exp", {}).get(r)])
                e_ok = X.act(act, prob[:, r, :], b.ap[:, 0:NK], ACT.Exp, bias=nmax[:, r:r + 1],
                             accum_out=psum_row[:, r:r + 1], after=[m_ok, T.get("prob_used", {}).get(r)])
                T.setdefault("exp", {})[r] = e_ok
                b.freed = [e_ok]
                i_ok = X.dve(nc.vector.reciprocal, prow_inv[:, r:r + 1], psum_row[:, r:r + 1],
                             after=[e_ok, T.get("inv_used", {}).get(r)])
                p_ok[n] = X.pool(pts, prob[:, r, :], prob[:, r, :], prow_inv[:, r:r + 1], None, ALU.mult, after=[i_ok])
                T.setdefault("inv_used", {})[r] = p_ok[n]

            def turn(n):
                h, i, r = n // TT, n % TT, n % NP
                b = ring_b.next()
                for j, (j0, m) in enumerate(JT):
                    t = X.pe(tr, b.ap[0:m, j * P:(j + 1) * P], prob[:, r, j0:j0 + m], ident[:, :],
                             signal=j == len(JT) - 1, after=b.freed + [p_ok[n]] if j == 0 else ())
                T.setdefault("prob_used", {})[r] = t
                src = b.ap[:, 0:len(JT) * P].rearrange("p (j i) -> p j i", j=len(JT))
                dst = probT[:, h % NP, :, i * P:(i + 1) * P]
                after = [t, T.get("probT_used", {}).get(h % NP)]
                pt_ok[n] = X.act(act, dst, src, ACT.Copy, after=after) if n % 2 else X.dve(cp, dst, src, after=after)
                b.freed = [pt_ok[n]]

            def values(q):
                b = ring_b.next()
                for j, (_, m) in enumerate(JT):
                    for e in range(2):
                        h = 2 * q + e
                        t = X.pe(mm, b.ap[e * HD:(e + 1) * HD, 0:L], V[0:m, j, h * HD:(h + 1) * HD],
                                 probT[0:m, h % NP, j, :], start=j == 0, stop=j == len(JT) - 1,
                                 signal=j == len(JT) - 1 and e == 1,
                                 after=b.freed + [T["V", s]] + [pt_ok[n] for n in range(4 * q, 4 * q + 4)]
                                 if j == 0 and e == 0 else ())
                for e in range(2):
                    T.setdefault("probT_used", {})[(2 * q + e) % NP] = t
                T["attn", s] = t
                t = X.act(act, oT[:, q, :], b.ap[:, 0:L], ACT.Copy, after=[t, tok("wo", s - 1)])
                b.freed = [t]
                return t

            for n in range(NU + LAG + 2):
                X.step(2000 if n < NU else 1500)
                if n < NU:
                    scores(n)
                if 0 <= n - LAG < NU:
                    turn(n - LAG)
                if n - LAG - 1 >= 0 and (n - LAG - 1) % 4 == 3:
                    o_ok = values((n - LAG - 1) // 4)

            X.step(3450)
            b = ring_b.next()
            for i in range(TT):
                for c in range(CT):
                    t = X.pe(mm, b.ap[:, i * D:(i + 1) * D], oT[:, c, i * P:(i + 1) * P], wo_sb[:, c, :], start=c == 0,
                             stop=c == CT - 1, signal=c == CT - 1, after=b.freed + [o_ok] if i == 0 and c == 0 else ())
            T["wo", s] = t
            t = X.dve(tt, x2[:, :, :], b.ap[:, :].rearrange("p (i d) -> p i d", i=TT), x1[:, s % 2, :, :], ALU.add,
                      after=[t])
            b.freed = [t]
            T["x1_used", s] = t
            n_t, mean, rstd = norm_stats(X, "att", [x2[:, i, :] for i in range(TT)], P, TT, [t])
            for i in range(TT):
                t = X.dve(ts, x2[:, i, :], x2[:, i, :], mean[i], rstd[i], ALU.subtract, ALU.mult,
                          after=[n_t, tok("x2T_pe", s - 1)])
            X.step(440)
            b = ring_b.next()
            for k in range(KT):
                for i in range(TT):
                    t_ok = X.pe(tr, b.ap[:, k * L + i * P:k * L + (i + 1) * P], x2[:, i, k * P:(k + 1) * P], ident[:, :],
                                after=b.freed + [t])
            T["x2T_pe", s] = t_ok
            for k in range(KT):
                t = X.act(act, x2T[:, s % 2, k, :], b.ap[:, k * L:(k + 1) * L], ACT.Copy,
                          accum_out=x2sum[:, s % 2, k:k + 1], after=[t_ok, tok("x2T_used", s - 2)])
            b.freed = [t]
            T["x2T", s] = t

        def ffn(s):
            i2 = s % 2
            ready_ = T["x2T", s]

            def glob():
                b = ring_c.next()
                for k in range(KT):
                    t = F.pe(mm, b.ap[:, 0:1], gw1_sb[:, k, :], x2sum[:, i2, k:k + 1], start=k == 0, stop=k == KT - 1,
                             signal=k == KT - 1, after=b.freed + [ready_])
                t = F.act(act, g1[:, :], b.ap[:, 0:1], ACT.Gelu, bias=prm("gc_b1"), scale=1.0 / L,
                          after=[t, tok("g1_used", s - 1)])
                b.freed = [t]
                yield
                b = ring_c.next()
                t = F.pe(mm, b.ap[0:HD, 0:1], gw2_sb[:, :], g1[:, :], start=True, stop=True, after=b.freed + [t])
                T["g1_used", s] = t
                t = F.act(act, g2[0:HD, :], b.ap[0:HD, 0:1], ACT.Gelu, bias=prm("gc_b2", 0, slice(0, HD)),
                          after=[t, tok("g2_used", s - 1)])
                b.freed = [t]
                yield
                b = ring_c.next()
                t = F.pe(mm, b.ap[:, 0:1], gw3_row[:, :], g2[:, :], start=True, stop=True, after=b.freed + [t])
                T["g2_used", s] = t
                t = F.act(act, tg[:, :], b.ap[:, 0:1], ACT.Tanh, bias=half_g3[:, :], scale=0.5, after=[t, tok("base", s - 1)])
                b.freed = [t]
                T["base", s] = F.dve(stt, c_cyc[:, :], tg[:, :], gf_gain[:, :], c_base[:, :], ALU.mult, ALU.add,
                                     after=[t, tok("cycles", s - 1)])

            gen = glob()
            cur = x2T[:, i2, :, :]
            for cyc in range(3):
                F.step(1730)
                if cyc == 0:
                    next(gen)
                b = ring_c.next()
                for m in range(KT):
                    for k in range(KT):
                        t = F.pe(mm, b.ap[:, m * L:(m + 1) * L], cw1_sb[:, k, m * P:(m + 1) * P], cur[:, k, :],
                                 start=k == 0, stop=k == KT - 1, signal=k == KT - 1,
                                 after=b.freed + [ready_] if m == 0 and k == 0 else ())
                for m in range(KT):
                    a = F.act(act, h1[:, m, :], b.ap[:, m * L:(m + 1) * L], ACT.Gelu, bias=prm("cn_b1", m), after=[t])
                b.freed = [a]
                F.step(860)
                if cyc == 0:
                    next(gen)
                b = ring_c.next()
                for k in range(KT):
                    t = F.pe(mm, b.ap[:, 0:L], cw2_sb[:, k, :], h1[:, k, :], start=k == 0, stop=k == KT - 1,
                             signal=k == KT - 1, after=b.freed + [a] if k == 0 else ())
                a = F.act(act, h2[:, :], b.ap[:, 0:L], ACT.Gelu, bias=prm("cn_b2"), after=[t])
                b.freed = [a]
                F.step(430)
                if cyc == 0:
                    for _ in gen:
                        pass
                b = ring_c.next()
                t = F.pe(mm, b.ap[0:HD, 0:L], cw3_sb[:, :], h2[:, :], start=True, stop=True, after=b.freed + [a])
                a = F.act(act, h3[0:HD, :], b.ap[0:HD, 0:L], ACT.Gelu, bias=prm("cn_b3", 0, slice(0, HD)), after=[t])
                b.freed = [a]
                F.step(430)
                b = ring_c.next()
                t = F.pe(mm, b.ap[:, 0:L], cw4_row[:, :], h3[:, :], start=True, stop=True, after=b.freed + [a])
                a = F.act(act, t4[:, :], b.ap[:, 0:L], ACT.Tanh, bias=half_b4[:, :], scale=0.5, after=[t])
                b.freed = [a]
                c_ok = F.dve(ts, cpl[:, :], t4[:, :], tf_gain[:, :], c_cyc[:, :], ALU.mult, ALU.add, after=[a, T["base", s]])
                w_ok = F.dve(tt, tw[:, :, :], cur, cpl[:, :].unsqueeze(1).broadcast_to([P, KT, L]), ALU.mult, after=[c_ok])
                nxt = f_cur[:, cyc % 2, :, :]
                F.dve(tt, nxt[:, 0, :], cur[:, 0, :], tw[:, 1, :], ALU.add, after=[w_ok, tok("fsum", s - 1)])
                ready_ = F.dve(tt, nxt[:, 1, :], cur[:, 1, :], tw[:, 0, :], ALU.subtract)
                cur = nxt
            T["cycles", s] = c_ok
            F.step(440)
            f_ok = F.dve(tt, f_sum[:, :, :], cur, x2T[:, i2, :, :], ALU.add, after=[ready_, tok("fsumT", s - 1)])
            T["fsum", s] = T["x2T_used", s] = f_ok
            b = ring_c.next()
            for i in range(TT):
                for k in range(KT):
                    t = F.pe(tr, b.ap[:, i * D + k * P:i * D + (k + 1) * P], f_sum[:, k, i * P:(i + 1) * P], ident[:, :],
                             after=b.freed + [f_ok])
            T["fsumT", s] = t
            n_t, mean, rstd = norm_stats(F, "ffn", [b.ap[:, i * D:(i + 1) * D] for i in range(TT)], P, TT, [t])
            stored = Token(s_out[i2], 16 * (s // 2)) if s >= 2 else None
            for i in range(TT):
                t = F.dve(ts, out_sb[:, i2, i, :], b.ap[:, i * D:(i + 1) * D], mean[i], rstd[i], ALU.subtract, ALU.mult,
                          after=[n_t, stored])
            b.freed = [t]
            F.steps[-1][1].append(("sp", [t], partial(nc.sync.dma_start, out[s].rearrange("(i p) d -> p i d", p=P),
                                                      out_sb[:, i2, :, :]), s_out[i2], 16))

        c_cyc = sb("c_cyc", [P, 1])

        queue = []
        queue += deal([S.take()])
        for p in range(NSEQ + 2):
            first, second = [], []
            loads.step(1)
            if p + 1 < NSEQ:
                load_seq(p + 1)
            if p < NSEQ:
                load_ctx(p)
            queue += deal([loads.take()])
            if p >= 2:
                ffn(p - 2)
                first.append(F.take())
            if 1 <= p <= NSEQ:
                attn_front(p - 1)
                first.append(X.take())
            if p < NSEQ:
                mixer_front(p)
                first.append(M.take())
            queue += deal(first)
            if p < NSEQ:
                mixer_dt(p)
                queue += deal([M.take()])
            if 1 <= p <= NSEQ:
                attn_back(p - 1)
                second.append(X.take())
            if p < NSEQ:
                mixer_back(p)
                second.append(M.take())
            queue += deal(second)

        def play(name, engine):
            passed = {}
            for who, after, build, s_, by in queue:
                if who != name:
                    continue
                need = {}
                for t in after:
                    if t.value > max(passed.get(id(t.sem), 0), need.get(id(t.sem), (0, None))[0]):
                        need[id(t.sem)] = (t.value, t.sem)
                for key, (value, sm) in need.items():
                    engine.wait_ge(sm, value)
                    passed[key] = value
                ins = build()
                if s_ is not None:
                    ins.then_inc(s_, by)

        block = es.enter_context(nc.Block())

        @block.tensor
        def _(e):
            play("pe", e)

        @block.scalar
        def _(e):
            play("act", e)

        @block.vector
        def _(e):
            play("dve", e)

        @block.gpsimd
        def _(e):
            play("pool", e)

        @block.sync
        def _(e):
            play("sp", e)
            for i in range(2):
                n = (NSEQ + 1 - i) // 2
                if n:
                    e.wait_ge(s_out[i], 16 * n)


def kernel(**inputs):
    import numpy as np
    import concourse.bacc as bacc
    from concourse import mybir
    from concourse.bass_utils import run_bass_kernel_spmd as run

    a = {k: np.asarray(v) for k, v in inputs.items()}
    P, DI, NS, H, HD = 128, 512, 16, 8, 64
    f32 = np.float32
    x = np.ascontiguousarray(a["x"])

    w = a["L0_attn_W_in"]
    w_in = np.zeros((w.shape[1], 2 * DI + TAIL), f32)
    w_in[:, 0:DI] = w[DI:2 * DI].T
    w_in[:, DI:2 * DI] = w[0:DI].T
    w_in[:, 2 * DI + ROW_B:2 * DI + ROW_B + NS] = w[2 * DI:2 * DI + NS].T
    w_in[:, 2 * DI + ROW_C:2 * DI + ROW_C + NS] = w[2 * DI + NS:2 * DI + 2 * NS].T
    w_in[:, 2 * DI + ROW_DT:2 * DI + ROW_DT + H] = w[2 * DI + 2 * NS:].T

    cols, n = param_columns()
    par = np.zeros((P, n), f32)
    cw = a["L0_attn_conv_w"][:, 0, :]
    cb = a["L0_attn_conv_b"]
    for c in range(4):
        par[:, cols["conv_w"][0] + 4 * c:cols["conv_w"][0] + 4 * c + 4] = cw[c * P:(c + 1) * P]
        par[:, cols["conv_b"][0] + c] = cb[c * P:(c + 1) * P]
        par[0:HD, cols["D"][0] + c] = a["L0_attn_D"][2 * c]
        par[HD:P, cols["D"][0] + c] = a["L0_attn_D"][2 * c + 1]
        par[:, cols["norm_w"][0] + c] = a["L0_attn_norm_w"][c * P:(c + 1) * P]
    for row, at in ((ROW_B, DI), (ROW_C, DI + NS)):
        par[row:row + NS, cols["conv_w"][0] + 16:cols["conv_w"][0] + 20] = cw[at:at + NS]
        par[row:row + NS, cols["conv_b"][0] + 4] = cb[at:at + NS]
    for name, key in (("ln_m_w", "L0_xattn_ln_m_w"), ("ln_m_b", "L0_xattn_ln_m_b"), ("ln_l_w", "L0_xattn_ln_l_w"),
                      ("ln_l_b", "L0_xattn_ln_l_b"), ("cn_b1", "L0_ffn_cn_b1")):
        par[:, cols[name][0]:cols[name][1]] = a[key].reshape(2, P).T
    par[:, cols["cn_b2"][0]] = a["L0_ffn_cn_b2"]
    par[0:HD, cols["cn_b3"][0]] = a["L0_ffn_cn_b3"]
    par[:, cols["cn_b4"][0]] = a["L0_ffn_cn_b4"][0]
    par[:, cols["gc_b1"][0]] = a["L0_ffn_gc_b1"]
    par[0:HD, cols["gc_b2"][0]] = a["L0_ffn_gc_b2"]
    par[:, cols["gc_b3"][0]] = a["L0_ffn_gc_b3"][0]
    par[:, cols["range"][0]] = a["L0_ffn_adaptive_range"][0]
    par[ROW_DT:ROW_DT + H, cols["dt_bias"][0]] = a["L0_attn_dt_bias"]
    par[ROW_DT:ROW_DT + H, cols["A_log"][0]] = a["L0_attn_A_log"]

    arrays = {
        "x": x, "xT": np.ascontiguousarray(x.transpose(0, 2, 1)), "ctx": a["ctx_1024"], "par": par, "w_in": w_in,
        "w_out": a["L0_attn_W_out"].T, "wq": a["L0_xattn_Wq"], "wkv": a["L0_xattn_Wkv"], "wo": a["L0_xattn_Wout"],
        "cw1": a["L0_ffn_cn_w1"], "cw2": a["L0_ffn_cn_w2"], "cw3": a["L0_ffn_cn_w3"], "cw4": a["L0_ffn_cn_w4"],
        "gw1": a["L0_ffn_gc_w1"], "gw2": a["L0_ffn_gc_w2"], "gw3": a["L0_ffn_gc_w3"],
    }
    arrays = {k: np.ascontiguousarray(v) for k, v in arrays.items()}
    nc = bacc.Bacc("TRN2", target_bir_lowering=False, num_devices=1)
    dram = [nc.dram_tensor(f"in_{k}", v.shape, mybir.dt.float32, kind="ExternalInput").ap() for k, v in arrays.items()]
    result = nc.dram_tensor("result", x.shape, mybir.dt.float32, kind="ExternalOutput").ap()
    decoder_layer(nc, *dram, result)
    r = run(nc, [{f"in_{k}": v for k, v in arrays.items()}], core_ids=[0])
    return r.results[0]["result"]
```

```python
from functools import partial
from itertools import zip_longest


class Token:

    def __init__(self, sem, value):
        self.sem, self.value = sem, value


class Lane:

    def __init__(self, program, stage, engine, sem):
        self.program, self.stage, self.engine, self.sem, self.count = program, stage, engine, sem, 0

    def __call__(self, build, *args, after=(), signal=True, by=1, sem=None, ns=None, table=None, **kw):
        if sem is None and signal:
            self.count += by
            done = Token(self.sem, self.count)
        else:
            done = sem
        self.program.append((self.stage, self.engine, [t for t in after if t], partial(build, *args, **kw),
                             done, by, ns or duration(self.engine, build, args, kw), table))
        return done


class Stage:

    def __init__(self, program, name, sems):
        self.pe, self.act, self.dve, self.pool, self.sp = (
            Lane(program, name, e, s) for e, s in zip(("pe", "act", "dve", "pool", "sp"), sems))


def duration(engine, build, args, kw):
    sizes, pointers, psum = [], 0, False
    for a in list(args) + list(kw.values()):
        if isinstance(a, (int, float, str, bool)) or a is None or "AP" not in type(a).__name__:
            continue
        n = 1
        for d in a.shape[1:]:
            n *= d
        sizes.append(n)
        pointers += n == 1
        psum = psum or a.name.startswith("bank")
    n, name = max(sizes, default=1), build.__name__
    if engine == "pe":
        if name == "transpose":
            return 2 * sizes[0] / 2.4
        passes = 4 if args[1].dtype == args[0].dtype else 1
        half = 0.55 if args[0].shape[0] == 64 and passes == 4 and sizes[0] > 200 else 1
        return 5 + passes * max(sizes[0], 12) / 2.4 * half
    if engine == "act":
        return (50 if psum else 93) + n / 1.2 + (93 if pointers else 0)
    if engine == "dve":
        rate = 1.92 if name in ("tensor_scalar", "tensor_copy") and not psum else 0.96
        return 65 + n / rate + (60 if pointers else 0)
    if engine == "pool":
        return 110 + n * 2.15 if n > 2 else 300 + 164 * n
    return 60


class Bank:

    def __init__(self, ap):
        self.ap, self.freed = ap, []


class Ring:

    def __init__(self, banks):
        self.banks, self.n = banks, 0

    def next(self):
        self.n += 1
        return self.banks[(self.n - 1) % len(self.banks)]


def order(program):
    AHEAD, SLACK = {"mixer_silu": 300, "mixer_y": 150, "attn_v": 300}, 0
    SWITCH = 1300
    HOP = {"pe": 197, "act": 150, "dve": 140, "pool": 80, "sp": 2000}
    lanes, phase_of, left, phase, last = {}, {}, {}, 0, None
    for i, op in enumerate(program):
        lanes.setdefault((op[1], op[0]), []).append(i)
        if op[7]:
            if op[7] != last:
                phase, last = phase + 1, op[7]
            phase_of[i] = phase
            left[phase] = left.get(phase, 0) + 1
    at = {k: 0 for k in lanes}
    free = {"pe": 0.0, "act": 0.0, "dve": 0.0, "pool": 0.0, "sp": 0.0}
    ended, queues, now_phase, count = {}, {e: [] for e in free}, 1, 0
    reached = {}

    def when(t):
        for value, time, engine in reached.get(id(t.sem), ()):
            if value >= t.value:
                return time, engine
        return None

    ready = {}
    total = len(program)
    while count < total:
        startable = []
        for key, idx in lanes.items():
            if at[key] >= len(idx):
                continue
            i = idx[at[key]]
            if i in phase_of and phase_of[i] != now_phase:
                continue
            if key not in ready:
                r = 0.0
                for t in program[i][2]:
                    w = when(t)
                    if w is None:
                        r = None
                        break
                    r = max(r, w[0] + (HOP[w[1]] if w[1] != key[0] else 50))
                if r is None:
                    continue
                ready[key] = r
            start = max(free[key[0]], ready[key])
            startable.append((start, i + AHEAD.get(key[1], 0), i, key))
        first = min(startable)[0] + SLACK
        start, _, i, key = min((c for c in startable if c[0] <= first), key=lambda c: c[1:3])
        stage, engine, after, build, done, by, ns, table = program[i]
        if i in phase_of:
            left[now_phase] -= 1
            if left[now_phase] == 0:
                now_phase += 1
                free[engine] += SWITCH
        free[engine] = max(start, free[engine]) + ns
        if done is not None:
            seq = reached.setdefault(id(done.sem), [])
            seq.append((done.value, free[engine], engine))
            if len(seq) > 400:
                del seq[:200]
        queues[engine].append(program[i])
        at[key] += 1
        ready.pop(key, None)
        count += 1
    return queues


def param_columns():
    names = [("conv_w", 20), ("conv_b", 5), ("D", 4), ("norm_w", 4), ("ln_m_w", 2), ("ln_m_b", 2),
             ("ln_l_w", 2), ("ln_l_b", 2), ("cn_b1", 2), ("cn_b2", 1), ("cn_b3", 1), ("cn_b4", 1),
             ("gc_b1", 1), ("gc_b2", 1), ("gc_b3", 1), ("range", 1), ("dt_bias", 1), ("A_log", 1)]
    cols, at = {}, 0
    for n, k in names:
        cols[n] = (at, at + k)
        at += k
    return cols, at


ROW_B, ROW_DT, ROW_C, TAIL = 0, 32, 64, 80


def decoder_layer(nc, x, xT, ctx_in, par_in, w_in, w_out, wq, wkv, wo, cw1, cw2, cw3, cw4, gw1, gw2, gw3, out):
    from contextlib import ExitStack
    from concourse import mybir

    F32, F32R, BF16 = mybir.dt.float32, mybir.dt.float32r, mybir.dt.bfloat16
    ALU, ACT, AX = mybir.AluOpType, mybir.ActivationFunctionType, mybir.AxisListType

    NSEQ, L, D = x.shape
    J = ctx_in.shape[1]
    P = 128
    KT = D // P
    TT = L // P
    H, HD, NS = 8, 64, 16
    DI = H * HD
    CT = DI // P
    NK = J + L
    JT = [(0, J)] + [(J + P * t, P) for t in range(TT)]
    TRI = L + P
    EPS = 1e-5
    cols, NPAR = param_columns()
    assert TT == 2 and KT == 2 and TRI == 384

    es = ExitStack()
    with es:
        def sb(name, shape, dt=F32):
            return es.enter_context(nc.sbuf_tensor(name, shape, dt))

        def sem(name):
            return es.enter_context(nc.semaphore(name))

        par = sb("par", [P, NPAR])

        def prm(name, i=0, rows=slice(0, P)):
            a = cols[name][0] + i
            return par[rows, a:a + 1]

        WIN = 2 * DI + TAIL
        w_in_hi, w_in_lo = sb("w_in_hi", [P, KT, WIN], F32R), sb("w_in_lo", [P, KT, WIN], F32R)
        wq_hi, wq_lo = sb("wq_hi", [P, KT, DI], F32R), sb("wq_lo", [P, KT, DI], F32R)
        wkv_hi, wkv_lo = sb("wkv_hi", [P, KT, 2 * DI], F32R), sb("wkv_lo", [P, KT, 2 * DI], F32R)
        w_out_sb, wo_sb = sb("w_out_sb", [P, CT, D]), sb("wo_sb", [P, CT, D])
        cw1_sb, cw2_sb = sb("cw1_sb", [P, KT, D]), sb("cw2_sb", [P, KT, P])
        cw3_sb, cw4_sb = sb("cw3_sb", [P, HD]), sb("cw4_sb", [P, 1])
        cw4_row = sb("cw4_row", [P, P])
        gw1_sb, gw2_sb = sb("gw1_sb", [P, KT, P]), sb("gw2_sb", [P, HD])
        gw3_sb, gw3_row = sb("gw3_sb", [P, 1]), sb("gw3_row", [P, P])
        ident, ones = sb("ident", [P, P]), sb("ones", [P, L])
        causal = sb("causal", [P, TRI])
        pick = sb("pick", [P, H, P], BF16)
        a_neg = sb("a_neg", [P, 1])
        minus_half = sb("minus_half", [P, TT])
        half_b4, half_g3 = sb("half_b4", [P, 1]), sb("half_g3", [P, 1])
        sign = sb("sign", [P, 1])
        tf_gain, gf_gain, c_base = sb("tf_gain", [P, 1]), sb("gf_gain", [P, 1]), sb("c_base", [P, 1])

        xT_sb, x_sb = sb("xT_sb", [P, 2, KT, L]), sb("x_sb", [P, 2, TT, D])
        ctx_sb = sb("ctx_sb", [P, 2, D])
        out_sb = sb("out_sb", [P, 2, TT, D])

        x_hi, x_lo = sb("x_hi", [P, KT, L], F32R), sb("x_lo", [P, KT, L], F32R)
        u, th = sb("u", [P, CT + 1, L]), sb("th", [P, CT + 1, L])
        xc, gate = sb("xc", [P, CT, L]), sb("gate", [P, CT, L])
        Bz, Cz = sb("Bz", [P, L]), sb("Cz", [P, L])
        dt_a, dt_e = sb("dt_a", [P, L]), sb("dt_e", [P, L])
        dc = sb("dc", [P, L])
        c_rest = sb("c_rest", [P, L])
        c_mid, c_parts = sb("c_mid", [P, L], BF16), sb("c_parts", [P, L], BF16)
        ncum, dt_tok = sb("ncum", [P, TT, H]), sb("dt_tok", [P, TT, H])
        G = sb("G", [P, TRI])
        Lm = sb("Lm", [P, H, TRI])
        xdt = sb("xdt", [P, TT, DI])
        g = sb("g", [P, CT, L])
        yD, sq = xc, gate
        ms, rms = sb("ms", [P, TT]), sb("rms", [P, TT])
        x1_pre, x1 = sb("x1_pre", [P, TT, D]), sb("x1", [P, 2, TT, D])

        ctx_n, x1_n = sb("ctx_n", [P, D]), sb("x1_n", [P, TT, D])
        kv, kv_hi, kv_lo = sb("kv", [P, KT, NK]), sb("kv_hi", [P, KT, NK], F32R), sb("kv_lo", [P, KT, NK], F32R)
        qT = sb("qT", [P, CT, L])
        kz = sb("kz", [P, H, NK])
        V = sb("V", [P, len(JT), DI])
        NP = 4
        prob, psum_row, prow_inv = sb("prob", [P, NP, NK]), sb("psum_row", [P, NP]), sb("prow_inv", [P, NP])
        nmax = sb("nmax", [P, NP])
        probT = sb("probT", [P, NP, len(JT), L])
        oT = sb("oT", [P, CT, L])
        x2 = sb("x2", [P, TT, D])
        x2T = sb("x2T", [P, KT, L])
        x2sum = sb("x2sum", [P, KT, TT])

        f_cur = sb("f_cur", [P, KT, L])
        h1, h2, h3 = sb("h1", [P, KT, L]), sb("h2", [P, L]), sb("h3", [P, L])
        t4, cpl, tw = sb("t4", [P, L]), sb("cpl", [P, L]), sb("tw", [P, KT, L])
        g1, g2, tg = sb("g1", [P, 1]), sb("g2", [P, 1]), sb("tg", [P, 1])
        f_sum = tw

        w_raw = Lm[:, :, :].rearrange("p h t -> p (h t)")[:, 0:KT * WIN].rearrange("p (k n) -> p k n", k=KT)
        wkv_raw = probT[:, :, :, :].rearrange("p a j t -> p (a j t)")[:, 0:KT * 2 * DI].rearrange("p (k n) -> p k n", k=KT)
        wq_raw = u[:, :, :].rearrange("p c t -> p (c t)")[:, 0:KT * DI].rearrange("p (k n) -> p k n", k=KT)

        stat = {n: (sb(f"st_{n}", [P, TT, 6]), sb(f"mv_{n}", [P, TT, 2]), sb(f"ve_{n}", [P, TT]),
                    sb(f"rs_{n}", [P, TT])) for n in ("mix", "ctx", "lat", "att", "ffn")}

        banks = [Bank(es.enter_context(nc.psum_tensor(f"bank{i}", [P, 512], F32))) for i in range(8)]
        ring_a, ring_b, ring_c = Ring(banks[0:3]), Ring(banks[3:5]), Ring(banks[5:8])

        program = []

        def stage(name):
            return Stage(program, name, [sem(f"{name}_{e}") for e in ("pe", "act", "dve", "pool", "sp")])

        S = stage("setup")
        I, M, MS, MD, MY = stage("mixer_in"), stage("mixer"), stage("mixer_silu"), stage("mixer_decay"), stage("mixer_y")
        X, XK, XW, XS, XN, XT, XV = (stage("attn"), stage("attn_v"), stage("attn_in"), stage("attn_scores"), stage("attn_norm"), stage("attn_turn"),
                             stage("attn_values"))
        F = [stage(f"ffn{i}") for i in range(TT)]
        LD, ST = stage("load"), stage("store")
        s_par, s_w = sem("s_par"), sem("s_w")
        s_x, s_ctx, s_out = ([sem(f"{n}{i}") for i in range(2)] for n in ("s_x", "s_ctx", "s_out"))
        mm, tr = nc.tensor.matmul, nc.tensor.transpose
        act = nc.scalar.activation
        ts, tt, stt, cp = (nc.vector.tensor_scalar, nc.vector.tensor_tensor,
                           nc.vector.scalar_tensor_tensor, nc.vector.tensor_copy)
        pts, ptt = nc.gpsimd.tensor_scalar, nc.gpsimd.tensor_tensor

        T = {}

        def tok(name, s):
            return T.get((name, s))

        loaded = [0]

        def load_w(dst, src):
            loaded[0] += 16
            return LD.sp(nc.sync.dma_start, dst, src, sem=Token(s_w, loaded[0]), by=16)

        par_in_tok = LD.sp(nc.sync.dma_start, par[:, :], par_in[:, :], sem=Token(s_par, 16), by=16)

        def load_seq(s):
            i, k = s % 2, s // 2 + 1
            LD.sp(nc.sync.dma_start, xT_sb[:, i, :, :], xT[s].rearrange("(k p) t -> p k t", p=P), by=16,
                  sem=Token(s_x[i], 32 * k - 16), after=[tok("xT_used", s - 2), tok("x_used", s - 2)])
            T["x_in", s] = LD.sp(nc.sync.dma_start, x_sb[:, i, :, :], x[s].rearrange("(k p) d -> p k d", p=P), by=16,
                                 sem=Token(s_x[i], 32 * k))

        def load_ctx(s):
            i, k = s % 2, s // 2 + 1
            T["ctx_in", s] = LD.sp(nc.sync.dma_start, ctx_sb[0:J, i, :], ctx_in[s], by=16, sem=Token(s_ctx[i], 16 * k),
                                   after=[tok("ctx_used", s - 2)])

        load_w(w_raw[:, :, :], w_in.rearrange("(k p) n -> p k n", p=P))
        load_seq(0)
        for dst, src in ((wq_raw[:, :, :], wq.rearrange("(k p) n -> p k n", p=P)),
                         (wkv_raw[:, :, :], wkv.rearrange("(k p) n -> p k n", p=P)),
                         (w_out_sb[:, :, :], w_out.rearrange("(k p) n -> p k n", p=P)),
                         (wo_sb[:, :, :], wo.rearrange("(k p) n -> p k n", p=P)),
                         (cw1_sb[:, :, :], cw1.rearrange("(k p) n -> p k n", p=P)),
                         (cw2_sb[:, :, :], cw2.rearrange("(k p) n -> p k n", p=P)),
                         (cw3_sb[:, :], cw3), (cw4_sb[0:HD, :], cw4),
                         (gw1_sb[:, :, :], gw1.rearrange("(k p) n -> p k n", p=P)),
                         (gw2_sb[:, :], gw2), (gw3_sb[0:HD, :], gw3)):
            w_tok = load_w(dst, src)

        pd, dv = S.pool, S.dve
        z_id = pd(nc.gpsimd.memset, ident[:, :], 0.0)
        z_ca = pd(nc.gpsimd.memset, causal[:, :], 1.0)
        z_pk = pd(nc.gpsimd.memset, pick[:, :, :], 0.0)
        id_ok = pd(nc.gpsimd.affine_select, out=ident[:, :], in_=ident[:, :], compare_op=ALU.not_equal, fill=1.0,
                   base=0, pattern=[[-1, P]], channel_multiplier=1, after=[z_id])
        for c0 in (0, L):
            z_ca = pd(nc.gpsimd.affine_select, out=causal[:, c0:c0 + P], in_=causal[:, c0:c0 + P],
                      compare_op=ALU.is_ge, fill=0.0, base=0, pattern=[[1, P]], channel_multiplier=-1, after=[z_ca])
        for r0 in (0, 32, 64):
            z_pk = pd(nc.gpsimd.affine_select, out=pick[:, :, :], in_=pick[:, :, :], compare_op=ALU.not_equal,
                      fill=1.0, base=-r0, pattern=[[-1, H], [0, P]], channel_multiplier=1, after=[z_pk])
        consts = [id_ok, z_ca, z_pk]
        dv(nc.vector.memset, ones[:, :], 1.0)
        for b in (Bz, Cz, dc, h3, gw3_row, cw4_row):
            dv(nc.vector.memset, b[:, :], 0.0)
        dv(nc.vector.memset, c_parts[:, :], 0.0)
        dv(nc.vector.memset, kz[:, :, :], 0.0)
        dv(nc.vector.memset, g2[:, :], 0.0)
        dv(nc.vector.memset, minus_half[:, :], -0.5)
        dv(nc.vector.memset, sign[0:64, :], 1.0)
        dv(nc.vector.memset, sign[64:P, :], -1.0)
        for b in banks:
            zeros = dv(nc.vector.memset, b.ap[:, :], 0.0)
        a0, a1 = cols["conv_w"][0], cols["conv_b"][1]
        dv(ts, par[:, a0:a1], par[:, a0:a1], 0.5, None, ALU.mult, after=[par_in_tok])
        dv(ts, half_b4[:, :], prm("cn_b4"), 0.5, None, ALU.mult)
        dv(ts, half_g3[:, :], prm("gc_b3"), 0.5, None, ALU.mult)
        dv(ts, tf_gain[:, :], prm("range"), sign[:, :], 0.3, ALU.mult, ALU.mult, after=[zeros])
        dv(ts, gf_gain[:, :], prm("range"), sign[:, :], 0.7, ALU.mult, ALU.mult)
        pars = dv(ts, c_base[:, :], sign[:, :], 0.1, None, ALU.mult)
        ea = S.act(act, a_neg[ROW_DT:ROW_DT + H, :], prm("A_log", 0, slice(ROW_DT, ROW_DT + H)), ACT.Exp, table="exp", after=[par_in_tok])
        pars2 = dv(ts, a_neg[ROW_DT:ROW_DT + H, :], a_neg[ROW_DT:ROW_DT + H, :], -1.0, None, ALU.mult, after=[ea])
        win = dv(ts, w_raw[:, :, DI:2 * DI], w_raw[:, :, DI:2 * DI], 0.5, None, ALU.mult, after=[w_tok])
        wqs = dv(ts, wq_raw[:, :, :], wq_raw[:, :, :], float(HD) ** -0.5, None, ALU.mult)
        for raw, hi, lo, t in ((w_raw, w_in_hi, w_in_lo, win), (wq_raw, wq_hi, wq_lo, wqs), (wkv_raw, wkv_hi, wkv_lo, None)):
            for k in range(KT):
                t = dv(cp, hi[:, k, :], raw[:, k, :], after=[t])
                w_split = dv(tt, lo[:, k, :], raw[:, k, :], hi[:, k, :].bitcast(F32), ALU.subtract, after=[t])
        for k in range(CT):
            dv(ts, w_out_sb[:, k, :], w_out_sb[:, k, :], prm("norm_w", k), None, ALU.mult)
        dv(ts, cw4_row[0:HD, :], ones[0:HD, 0:P], cw4_sb[0:HD, :], None, ALU.mult)
        w_ready = dv(ts, gw3_row[0:HD, :], ones[0:HD, 0:P], gw3_sb[0:HD, :], None, ALU.mult)
        ready = [w_ready] + consts
        T["setup"] = ready

        def norm_stats(st, name, src, rows, after, first=0):
            stats, mv, ve, rs = stat[name]
            tiles = range(first, first + len(src))
            c = slice(first, first + len(src))
            for i, a in zip(tiles, src):
                t = st.dve(nc.vector.bn_stats, stats[0:rows, i, :], a, after=after)
            for i in tiles:
                t = st.dve(nc.vector.bn_aggr, mv[0:rows, i, :], stats[0:rows, i, :], after=[t])
            t = st.pool(pts, ve[0:rows, c], mv[0:rows, c, 1], EPS, None, ALU.add, after=[t])
            t = st.pool(ptt, rs[0:rows, c], ve[0:rows, c], minus_half[0:rows, c], ALU.pow, after=[t])
            return t, [mv[0:rows, i, 0:1] for i in tiles], [rs[0:rows, i:i + 1] for i in tiles]

        def product3(st, dst, w_hi, w_lo, x_hi_, x_lo_, after, x_is_rhs=True):
            n = 0
            for k in range(KT):
                for w_, x_ in ((w_hi[k], x_hi_[k]), (w_lo[k], x_hi_[k]), (w_hi[k], x_lo_[k])):
                    a, b = (w_, x_) if x_is_rhs else (x_, w_)
                    n += 1
                    t = st.pe(mm, dst, a, b, start=n == 1, stop=n == 3 * KT, signal=n == 3 * KT,
                              after=after if n == 1 else ())
            return t

        def project(dst, c0, n, after):
            return product3(I, dst, [w_in_hi[:, k, c0:c0 + n] for k in range(KT)],
                            [w_in_lo[:, k, c0:c0 + n] for k in range(KT)],
                            [x_hi[:, k, :] for k in range(KT)], [x_lo[:, k, :] for k in range(KT)], after)

        def conv(s, src, c, rows, ready_):
            return I.act(act, u[0:rows, c, :], src, ACT.Identity, scale=prm("conv_w", 4 * c + 3, slice(0, rows)),
                         bias=prm("conv_b", c, slice(0, rows)), after=[ready_, tok("conv", s - 1)])

        def taps(src, c, rows, after):
            for d in (1, 2, 3):
                after = [I.dve(stt, u[0:rows, c, d:L], src[:, 0:L - d], prm("conv_w", 4 * c + 3 - d, slice(0, rows)),
                               u[0:rows, c, d:L], ALU.mult, ALU.add, after=after)]
            return after[0]

        def mixer_head(s):
            i = s % 2
            hi_ok = I.act(act, x_hi[:, :, :], xT_sb[:, i, :, :], ACT.Copy,
                          after=[tok("x_in", s), tok("in_proj", s - 1)])
            lo_ok = I.dve(tt, x_lo[:, :, :], xT_sb[:, i, :, :], x_hi[:, :, :].bitcast(F32), ALU.subtract, after=[hi_ok])
            T["xT_used", s] = lo_ok
            T["x_split", s] = [hi_ok, lo_ok]

            b = ring_c.next()
            p_ok = project(b.ap[0:TAIL, 0:L], 2 * DI, TAIL, b.freed + T["setup"] + [hi_ok, lo_ok])
            c_ok = conv(s, b.ap[0:TAIL, 0:L], CT, TAIL, p_ok)
            u_ok = taps(b.ap[0:TAIL, 0:L], CT, TAIL, [c_ok])
            a_ok = I.dve(ts, dt_a[ROW_DT:ROW_DT + H, :], b.ap[ROW_DT:ROW_DT + H, 0:L],
                         prm("dt_bias", 0, slice(ROW_DT, ROW_DT + H)), None, ALU.add,
                         after=[p_ok, tok("dt", s - 1)])
            T["dt_a", s] = a_ok
            b.freed = [a_ok]
            t_ok = MS.act(act, th[0:TAIL, CT, :], u[0:TAIL, CT, :], ACT.Tanh, after=[u_ok, tok("BC", s - 1)])
            MS.dve(stt, Bz[0:NS, :], th[0:NS, CT, :], 1.0, u[0:NS, CT, :], ALU.add, ALU.mult,
                  after=[t_ok, tok("CB", s - 1)])
            T["BC", s] = MS.dve(stt, Cz[0:NS, :], th[ROW_C:ROW_C + NS, CT, :], 1.0, u[ROW_C:ROW_C + NS, CT, :],
                               ALU.add, ALU.mult)

        def mixer_front(s):
            for j in range(CT // 2):
                b = ring_c.next()
                aps = [b.ap[:, 0:L], b.ap[:, L:2 * L]]
                after = b.freed + T["x_split", s]
                for e in range(2):
                    p_ok = project(aps[e], (2 * j + e) * P, P, after)
                    after = []
                c_ok = [conv(s, aps[e], 2 * j + e, P, p_ok) for e in range(2)]
                u_ok = [taps(aps[e], 2 * j + e, P, c_ok) for e in range(2)]
                b.freed = [u_ok[1]]
                t_ok = MS.act(act, th[:, 2 * j:2 * j + 2, :], u[:, 2 * j:2 * j + 2, :], ACT.Tanh, after=u_ok + [tok("gate", s - 1)])
                T["xc", s] = MS.dve(stt, xc[:, 2 * j:2 * j + 2, :], th[:, 2 * j:2 * j + 2, :], 1.0,
                                   u[:, 2 * j:2 * j + 2, :], ALU.add, ALU.mult, after=[t_ok, tok("xc_used", s - 1)])
            T["conv", s] = T["xc", s]
            for j in range(CT // 2):
                b = ring_c.next()
                after = b.freed
                for e in range(2):
                    p_ok = project(b.ap[:, e * L:(e + 1) * L], DI + (2 * j + e) * P, P, after)
                    after = []
                flat = b.ap[:, :].rearrange("p (e t) -> p e t", e=2)
                t_ok = MS.act(act, th[:, 2 * j:2 * j + 2, :], flat, ACT.Tanh, after=[p_ok, T["xc", s]])
                g_ok = MS.dve(stt, gate[:, 2 * j:2 * j + 2, :], th[:, 2 * j:2 * j + 2, :], 1.0, flat, ALU.add, ALU.mult,
                             after=[t_ok, tok("ms", s - 1)])
                b.freed = [g_ok]
            T["gate", s] = g_ok
            T["in_proj", s] = p_ok

        def mixer_softplus(s):
            r = slice(ROW_DT, ROW_DT + H)
            n_ok = M.dve(stt, dt_e[r, :], dt_a[r, :], -1.0, dt_a[r, :], ALU.mult, ALU.min, after=[T["dt_a", s]])
            e_ok = M.act(act, dt_e[r, :], dt_e[r, :], ACT.Exp, table="exp", after=[n_ok])
            l_ok = M.act(act, dt_e[r, :], dt_e[r, :], ACT.Ln, table="ln", bias=ones[r, 0:1], after=[e_ok])
            T["ln", s] = l_ok

        def mixer_prep(s):
            r = slice(ROW_DT, ROW_DT + H)
            d_ok = M.dve(stt, dc[r, :], dt_a[r, :], 0.0, dt_e[r, :], ALU.max, ALU.add,
                         after=[T["ln", s], tok("dc_used", s - 1)])
            T["dt", s] = d_ok
            a_ok = M.dve(ts, dt_e[r, :], dc[r, :], a_neg[r, :], None, ALU.mult, after=[d_ok])
            c_ok = M.dve(nc.vector.tensor_tensor_scan, dc[0:H, :], ones[r, :], dt_e[r, :], 0.0, ALU.mult, ALU.add,
                         after=[a_ok])
            t = M.pool(pts, c_parts[0:H, :], dc[0:H, :], 1.0, None, ALU.mult, after=[c_ok, tok("parts_used", s - 1)])
            t = M.pool(ptt, c_rest[0:H, :], dc[0:H, :], c_parts[0:H, :], ALU.subtract, after=[t])
            t = M.pool(pts, c_mid[0:H, :], c_rest[0:H, :], 1.0, None, ALU.mult, after=[t])
            M.dve(cp, c_parts[32:32 + H, :], c_rest[0:H, :], after=[t])
            T["parts", s] = M.dve(tt, c_parts[64:64 + H, :], c_rest[0:H, :], c_mid[0:H, :], ALU.subtract)
            T["cum", s] = c_ok

            b = ring_c.next()
            for i in range(TT):
                t = M.pe(tr, b.ap[:, i * 64:i * 64 + 40], dc[0:40, i * P:(i + 1) * P], ident[0:40, 0:40],
                         after=b.freed + [T["cum", s]])
            T["dc_used", s] = t
            bt = b.ap[:, 0:64 * TT].rearrange("p (i c) -> p i c", i=TT)
            n_ok = M.dve(ts, ncum[:, :, :], bt[:, :, 0:H], -1.0, None, ALU.mult, after=[t, tok("decay_all", s - 1)])
            d_ok = M.dve(cp, dt_tok[:, :, :], bt[:, :, 32:32 + H], after=[tok("xdt", s - 1)])
            b.freed = [d_ok]

            b = ring_c.next()
            M.pe(mm, b.ap[:, 0:L], Bz[:, 0:P], Cz[:, :], start=True, stop=True, after=b.freed + [T["BC", s]], signal=False)
            t = M.pe(mm, b.ap[:, L:TRI], Bz[:, P:L], Cz[:, P:L], start=True, stop=True)
            T["CB", s] = t
            G_ok = M.dve(tt, G[:, :], b.ap[:, 0:TRI], causal[:, :], ALU.mult, after=[t, tok("Lm", s - 1)])
            b.freed = [G_ok]

            def exponents(q):
                b = ring_c.next()
                for e in range(2):
                    t = MD.pe(mm, b.ap[:, e * L:(e + 1) * L], pick[:, 2 * q + e, :], c_parts[:, :], start=True, stop=True,
                             signal=e == 1, after=b.freed + [T["parts", s]] if e == 0 else ())
                T["parts_used", s] = t
                for e in range(2):
                    h = 2 * q + e
                    for i, c0, c1, m0 in ((0, 0, L, 0), (1, P, L, L)):
                        x_ok = MD.dve(ts, Lm[:, h, m0:m0 + c1 - c0], b.ap[:, e * L + c0:e * L + c1], ncum[:, i, h:h + 1],
                                     0.0, ALU.add, ALU.min, after=[t, n_ok, tok("y", s - 1)])
                b.freed = [x_ok]
                return x_ok

            T["G", s], T["dt_tok", s] = G_ok, d_ok
            T["decay", s] = [exponents(q) for q in range(CT)]
            T["decay_all", s] = T["decay", s][-1]

        def mixer_back(s):
            for i in range(TT):
                b = ring_c.next()
                for c in range(CT):
                    t = M.pe(tr, b.ap[:, c * P:(c + 1) * P], xc[:, c, i * P:(i + 1) * P], ident[:, :], signal=c == CT - 1,
                             after=b.freed + [T["xc", s]] if c == 0 else ())
                xdt_ok = M.dve(tt, xdt[:, i, :].rearrange("p (h d) -> p h d", h=H), b.ap[:, :].rearrange("p (h d) -> p h d", h=H),
                               dt_tok[:, i, :].unsqueeze(2).broadcast_to([P, H, HD]), ALU.mult,
                               after=[t, T["dt_tok", s], tok("y", s - 1)])
                b.freed = [xdt_ok]
            T["xdt", s] = xdt_ok

            def decay(q):
                pair = Lm[:, 2 * q:2 * q + 2, :]
                e_ok = MD.act(act, pair, pair, ACT.Exp, table="exp", after=[T["decay", s][q]])
                return MD.pool(ptt, pair, pair, G[:, :].unsqueeze(1).broadcast_to([P, 2, TRI]), ALU.mult,
                               after=[e_ok, T["G", s]])

            def y_pair(q, lm_ok):
                b = ring_c.next()
                for i, (c0, c1, m0) in enumerate(((0, L, 0), (P, L, L))):
                    for e in range(2):
                        h = 2 * q + e
                        t = MY.pe(mm, b.ap[e * HD:(e + 1) * HD, c0:c1], xdt[:, i, h * HD:(h + 1) * HD],
                                 Lm[:, h, m0:m0 + c1 - c0], start=i == 0, stop=i == 1, signal=i == 1 and e == 1,
                                 after=b.freed + [lm_ok, xdt_ok] if i == 0 and e == 0 else ())
                T["y", s] = t
                y_ok = MY.dve(stt, yD[:, q, :], xc[:, q, :], prm("D", q), b.ap[:, 0:L], ALU.mult, ALU.add,
                             after=[t])
                b.freed = [y_ok]
                g_ok = MY.pool(ptt, g[:, q, :], yD[:, q, :], gate[:, q, :], ALU.mult,
                              after=[y_ok, tok("gate", s), tok("out_proj", s - 1)])
                T["xc_used", s] = g_ok
                return g_ok, MY.act(act, sq[:, q, :], g[:, q, :], ACT.Square, after=[g_ok, tok("gate", s)])

            lm_ok = {}
            for q in range(CT + 2):
                if q < CT:
                    T["Lm", s] = lm_ok[q] = decay(q)
                if q > 1:
                    g_ok, sq_ok = y_pair(q - 2, lm_ok[q - 2])

            t = M.pool(ptt, sq[:, 0:2, :], sq[:, 0:2, :], sq[:, 2:4, :], ALU.add, after=[sq_ok])
            t = M.pool(ptt, sq[:, 0, :], sq[:, 0, :], sq[:, 1, :], ALU.add, after=[t])
            b2 = ring_c.next()
            for i in range(TT):
                for c in range(CT):
                    o_ok = M.pe(mm, b2.ap[:, i * D:(i + 1) * D], g[:, c, i * P:(i + 1) * P], w_out_sb[:, c, :],
                                start=c == 0, stop=c == CT - 1, signal=c == CT - 1,
                                after=b2.freed + [g_ok] if i == 0 and c == 0 else ())
            T["out_proj", s] = o_ok
            b = ring_c.next()
            for i in range(TT):
                m_ok = M.pe(mm, b.ap[:, 2 * i:2 * i + 2], sq[:, 0, i * P:(i + 1) * P], ones[:, 0:2], start=True, stop=True,
                            after=b.freed + [t])
            v_ok = M.dve(ts, ms[:, :], b.ap[:, 0:2 * TT].rearrange("p (i c) -> p i c", c=2)[:, :, 0], 1.0 / DI, EPS,
                         ALU.mult, ALU.add, after=[m_ok, tok("rms", s - 1)])
            b.freed = [v_ok]
            T["ms", s] = m_ok
            r_ok = M.pool(ptt, rms[:, :], ms[:, :], minus_half[:, :], ALU.pow, after=[v_ok, tok("x_used", s - 1)])
            T["rms", s] = r_ok
            for i in range(TT):
                t = M.dve(stt, x1_pre[:, i, :], b2.ap[:, i * D:(i + 1) * D], rms[:, i:i + 1], x_sb[:, s % 2, i, :],
                          ALU.mult, ALU.add, after=[r_ok, o_ok])
            b2.freed = [t]
            T["x_used", s] = t
            n_t, mean, rstd = norm_stats(M, "mix", [x1_pre[:, i, :] for i in range(TT)], P, [t])
            for i in range(TT):
                t = M.dve(ts, x1[:, s % 2, i, :], x1_pre[:, i, :], mean[i], rstd[i], ALU.subtract, ALU.mult,
                          after=[n_t, tok("x1_used", s - 2)])
            T["x1", s] = t
            n_t, mean, rstd = norm_stats(M, "lat", [x1[:, s % 2, i, :] for i in range(TT)], P, [T["x1", s]])
            for i in range(TT):
                t = M.dve(ts, x1_n[:, i, :], x1[:, s % 2, i, :], mean[i], rstd[i], ALU.subtract, ALU.mult,
                          after=[n_t, tok("x1T", s - 1)])
            T["x1_n", s] = t

        def attn_context(s):
            i2 = s % 2
            n_t, mean, rstd = norm_stats(XK, "ctx", [ctx_sb[0:J, i2, :]], J, [tok("ctx_in", s)])
            t = XK.dve(ts, ctx_n[0:J, :], ctx_sb[0:J, i2, :], mean[0], rstd[0], ALU.subtract, ALU.mult,
                      after=[n_t, tok("ctxT", s - 1)])
            T["ctx_used", s] = t
            b = ring_c.next()
            for k in range(KT):
                c_ok = XK.pe(tr, b.ap[:, k * J:(k + 1) * J], ctx_n[0:J, k * P:(k + 1) * P], ident[0:J, 0:J],
                            after=b.freed + [t] + T["setup"])
            T["ctxT", s] = c_ok
            for k in range(KT):
                kv_c = XK.act(act, kv[:, k, 0:J], b.ap[:, k * J:(k + 1) * J], ACT.Identity, scale=prm("ln_m_w", k),
                             bias=prm("ln_m_b", k), after=[c_ok, tok("kv_used", s - 1)])
            b.freed = [kv_c]
            T["kv_c", s] = kv_c

        def attn_keys_in(s):
            b = ring_c.next()
            for k in range(KT):
                for i in range(TT):
                    l_ok = XK.pe(tr, b.ap[:, k * L + i * P:k * L + (i + 1) * P], x1_n[:, i, k * P:(k + 1) * P], ident[:, :],
                                after=b.freed + [T["x1_n", s]])
            T["x1T", s] = l_ok
            for k in range(KT):
                kv_l = XK.act(act, kv[:, k, J:NK], b.ap[:, k * L:(k + 1) * L], ACT.Identity, scale=prm("ln_l_w", k),
                             bias=prm("ln_l_b", k), after=[l_ok])
            b.freed = [kv_l]
            hi_ok = XK.act(act, kv_hi[:, :, :], kv[:, :, :], ACT.Copy, after=[kv_l, T["kv_c", s], tok("proj", s - 1)])
            lo_ok = XK.dve(tt, kv_lo[:, :, :], kv[:, :, :], kv_hi[:, :, :].bitcast(F32), ALU.subtract, after=[hi_ok])
            T["kv_used", s] = lo_ok
            T["kv", s] = [hi_ok, lo_ok]

        def attn_front(s):
            i2 = s % 2
            x_ok = T["kv", s]

            def q_pair(j):
                b = ring_b.next()
                after = b.freed + x_ok
                for e in range(2):
                    c0 = (2 * j + e) * P
                    p_ok = product3(X, b.ap[:, e * L:(e + 1) * L], [wq_hi[:, k, c0:c0 + P] for k in range(KT)],
                                    [wq_lo[:, k, c0:c0 + P] for k in range(KT)], [kv_hi[:, k, J:NK] for k in range(KT)],
                                    [kv_lo[:, k, J:NK] for k in range(KT)], after)
                    after = []
                t = X.act(act, qT[:, 2 * j:2 * j + 2, :], b.ap[:, :].rearrange("p (e t) -> p e t", e=2), ACT.Copy,
                          after=[p_ok, tok("scores", s - 1)])
                b.freed = [t]
                T["qT", s, j] = t

            def k_tile(c):
                b = ring_b.next()
                p_ok = product3(X, b.ap[:, 0:NK], [wkv_hi[:, k, c * P:(c + 1) * P] for k in range(KT)],
                                [wkv_lo[:, k, c * P:(c + 1) * P] for k in range(KT)], [kv_hi[:, k, :] for k in range(KT)],
                                [kv_lo[:, k, :] for k in range(KT)], b.freed + x_ok)
                t1 = X.act(act, kz[0:HD, 2 * c, :], b.ap[0:HD, 0:NK], ACT.Copy, after=[p_ok, tok("scores", s - 1)])
                t2 = X.dve(cp, kz[HD:P, 2 * c + 1, :], b.ap[HD:P, 0:NK], after=[p_ok, tok("scores", s - 1)])
                b.freed = [t1, t2]
                T["kz", s, c] = [t1, t2]

            def v_tile(j):
                j0, n = JT[j]
                b = ring_b.next()
                p_ok = product3(XW, b.ap[0:n, :], [wkv_hi[:, k, DI:2 * DI] for k in range(KT)],
                                [wkv_lo[:, k, DI:2 * DI] for k in range(KT)], [kv_hi[:, k, j0:j0 + n] for k in range(KT)],
                                [kv_lo[:, k, j0:j0 + n] for k in range(KT)], b.freed + x_ok, x_is_rhs=False)
                t = XW.act(act, V[0:n, j, :], b.ap[0:n, :], ACT.Copy, after=[p_ok, tok("attn", s - 1)])
                b.freed = [t]
                T["V", s] = t
                T["proj", s] = p_ok

            for j in range(CT // 2):
                q_pair(j)
            for c in range(CT):
                k_tile(c)
            for j in range(len(JT)):
                v_tile(j)

        def attn_back(s):
            NU, LAG = H * TT, 3
            p_ok, pt_ok, o_ok = {}, {}, None

            def scores(n):
                h, i, r = n // TT, n % TT, n % NP
                b = ring_a.next()
                t = XS.pe(mm, b.ap[:, 0:NK], qT[:, h // 2, i * P:(i + 1) * P], kz[:, h, :], start=True, stop=True,
                         after=b.freed + [T["qT", s, h // 4]] + T["kz", s, h // 2])
                T["scores", s] = t
                m_ok = XS.dve(nc.vector.tensor_reduce, nmax[:, r:r + 1], b.ap[:, 0:NK], AX.X, ALU.max, negate=True,
                             after=[t, T.get("exp", {}).get(r)])
                e_ok = XS.act(act, prob[:, r, :], b.ap[:, 0:NK], ACT.Exp, table="exp", bias=nmax[:, r:r + 1],
                             accum_out=psum_row[:, r:r + 1], after=[m_ok, T.get("prob_used", {}).get(r)])
                T.setdefault("exp", {})[r] = e_ok
                b.freed = [e_ok]
                i_ok = XN.dve(nc.vector.reciprocal, prow_inv[:, r:r + 1], psum_row[:, r:r + 1],
                             after=[e_ok, T.get("inv_used", {}).get(r)])
                p_ok[n] = XN.dve(ts, prob[:, r, :], prob[:, r, :], prow_inv[:, r:r + 1], None, ALU.mult, after=[i_ok])
                T.setdefault("inv_used", {})[r] = p_ok[n]

            def turn(n):
                h, i, r = n // TT, n % TT, n % NP
                b = ring_b.next()
                for j, (j0, m) in enumerate(JT):
                    t = XT.pe(tr, b.ap[0:m, j * P:(j + 1) * P], prob[:, r, j0:j0 + m], ident[:, :],
                             signal=j == len(JT) - 1, after=b.freed + [p_ok[n]] if j == 0 else ())
                T.setdefault("prob_used", {})[r] = t
                src = b.ap[:, 0:len(JT) * P].rearrange("p (j i) -> p j i", j=len(JT))
                dst = probT[:, h % NP, :, i * P:(i + 1) * P]
                after = [t, T.get("probT_used", {}).get(h % NP)]
                pt_ok[n] = XT.act(act, dst, src, ACT.Copy, after=after) if n % 4 else XT.dve(cp, dst, src, after=after)
                b.freed = [pt_ok[n]]

            def values(q):
                b = ring_b.next()
                for j, (_, m) in enumerate(JT):
                    for e in range(2):
                        h = 2 * q + e
                        t = XV.pe(mm, b.ap[e * HD:(e + 1) * HD, 0:L], V[0:m, j, h * HD:(h + 1) * HD],
                                 probT[0:m, h % NP, j, :], start=j == 0, stop=j == len(JT) - 1,
                                 signal=j == len(JT) - 1 and e == 1,
                                 after=b.freed + [T["V", s]] + [pt_ok[n] for n in range(4 * q, 4 * q + 4)]
                                 if j == 0 and e == 0 else ())
                for e in range(2):
                    T.setdefault("probT_used", {})[(2 * q + e) % NP] = t
                T["attn", s] = t
                t = XV.act(act, oT[:, q, :], b.ap[:, 0:L], ACT.Copy, after=[t, tok("wo", s - 1)])
                b.freed = [t]
                return t

            for n in range(NU + LAG + 2):
                if n < NU:
                    scores(n)
                if 0 <= n - LAG < NU:
                    turn(n - LAG)
                if n - LAG - 1 >= 0 and (n - LAG - 1) % 4 == 3:
                    o_ok = values((n - LAG - 1) // 4)

            for i in range(TT):
                b = ring_b.next()
                for c in range(CT):
                    t = XV.pe(mm, b.ap[:, 0:D], oT[:, c, i * P:(i + 1) * P], wo_sb[:, c, :], start=c == 0,
                             stop=c == CT - 1, signal=c == CT - 1, after=b.freed + [o_ok] if c == 0 else ())
                T["x2_pre", s, i] = XV.dve(tt, x2[:, i, :], b.ap[:, 0:D], x1[:, s % 2, i, :], ALU.add,
                                           after=[t, T.get(("x2T_pe", s - 1, i))])
                b.freed = [T["x2_pre", s, i]]
            T["wo", s] = t
            T["x1_used", s] = T["x2_pre", s, TT - 1]


        def ffn(s):
            i2 = s % 2
            x2T_ok, base = {}, {}

            def glob():
                st, b = F[TT - 1], banks[TT - 1]
                for k in range(KT):
                    for i in range(TT):
                        t = st.pe(mm, b.ap[:, 0:1], gw1_sb[:, k, :], x2sum[:, k, i:i + 1], start=k + i == 0,
                                  stop=k + i == KT + TT - 2, signal=k + i == KT + TT - 2,
                                  after=b.freed + [x2T_ok[n] for n in range(TT)])
                T["x2sum_used", s] = t
                t = st.act(act, g1[:, :], b.ap[:, 0:1], ACT.Gelu, table="gelu", bias=prm("gc_b1"), scale=1.0 / L,
                           after=[t, tok("g1_used", s - 1)])
                b.freed = [t]
                yield
                t = st.pe(mm, b.ap[0:HD, 0:1], gw2_sb[:, :], g1[:, :], start=True, stop=True, after=b.freed + [t])
                T["g1_used", s] = t
                t = st.act(act, g2[0:HD, :], b.ap[0:HD, 0:1], ACT.Gelu, table="gelu", bias=prm("gc_b2", 0, slice(0, HD)),
                           after=[t, tok("g2_used", s - 1)])
                b.freed = [t]
                yield
                t = st.pe(mm, b.ap[:, 0:1], gw3_row[:, :], g2[:, :], start=True, stop=True, after=b.freed + [t])
                T["g2_used", s] = t
                t = st.act(act, tg[:, :], b.ap[:, 0:1], ACT.Tanh, bias=half_g3[:, :], scale=0.5, after=[t, tok("base", s - 1)])
                b.freed = [t]
                T["base", s] = st.dve(stt, c_cyc[:, :], tg[:, :], gf_gain[:, :], c_base[:, :], ALU.mult, ALU.add,
                                      after=[t] + [T.get(("cycles", s - 1, n)) for n in range(TT)])
                yield

            def chain(i, gen):
                st, b = F[i], banks[i]
                cols_ = slice(i * P, (i + 1) * P)
                n_t, mean, rstd = norm_stats(st, "att", [x2[:, i, :]], P, [T["x2_pre", s, i]], first=i)
                t = st.dve(ts, x2[:, i, :], x2[:, i, :], mean[0], rstd[0], ALU.subtract, ALU.mult, after=[n_t])
                yield
                for k in range(KT):
                    t_ok = st.pe(tr, b.ap[:, k * P:(k + 1) * P], x2[:, i, k * P:(k + 1) * P], ident[:, :],
                                 after=b.freed + [t])
                T["x2T_pe", s, i] = t_ok
                for k in range(KT):
                    t = st.act(act, x2T[:, k, cols_], b.ap[:, k * P:(k + 1) * P], ACT.Copy,
                               accum_out=x2sum[:, k, i:i + 1],
                               after=[t_ok, T.get(("fsum", s - 1, i)), tok("x2sum_used", s - 1)])
                b.freed = [t]
                x2T_ok[i] = ready_ = t
                yield
                cur, nxt = x2T[:, :, cols_], f_cur[:, :, cols_]
                for cyc in range(3):
                    for m in range(KT):
                        for k in range(KT):
                            t = st.pe(mm, b.ap[:, m * P:(m + 1) * P], cw1_sb[:, k, m * P:(m + 1) * P], cur[:, k, :],
                                      start=k == 0, stop=k == KT - 1, signal=k == KT - 1,
                                      after=b.freed + [ready_] if m == 0 and k == 0 else ())
                    for m in range(KT):
                        a = st.act(act, h1[:, m, cols_], b.ap[:, m * P:(m + 1) * P], ACT.Gelu, table="gelu",
                                   bias=prm("cn_b1", m), after=[t])
                    b.freed = [a]
                    yield
                    for _ in zip(gen, (0,)) if cyc == 0 else ():
                        pass
                    for k in range(KT):
                        t = st.pe(mm, b.ap[:, 0:P], cw2_sb[:, k, :], h1[:, k, cols_], start=k == 0, stop=k == KT - 1,
                                  signal=k == KT - 1, after=b.freed + [a] if k == 0 else ())
                    a = st.act(act, h2[:, cols_], b.ap[:, 0:P], ACT.Gelu, table="gelu", bias=prm("cn_b2"), after=[t])
                    b.freed = [a]
                    yield
                    for _ in zip(gen, (0,)) if cyc == 0 else ():
                        pass
                    t = st.pe(mm, b.ap[0:HD, 0:P], cw3_sb[:, :], h2[:, cols_], start=True, stop=True, after=b.freed + [a])
                    a = st.act(act, h3[0:HD, cols_], b.ap[0:HD, 0:P], ACT.Gelu, table="gelu",
                               bias=prm("cn_b3", 0, slice(0, HD)), after=[t])
                    b.freed = [a]
                    yield
                    for _ in gen if cyc == 0 else ():
                        pass
                    t = st.pe(mm, b.ap[:, 0:P], cw4_row[:, :], h3[:, cols_], start=True, stop=True, after=b.freed + [a])
                    a = st.act(act, t4[:, cols_], b.ap[:, 0:P], ACT.Tanh, bias=half_b4[:, :], scale=0.5, after=[t])
                    b.freed = [a]
                    yield
                    c_ok = st.dve(ts, cpl[:, cols_], t4[:, cols_], tf_gain[:, :], c_cyc[:, :], ALU.mult, ALU.add,
                                  after=[a, T["base", s]])
                    w_ok = st.dve(tt, tw[:, :, cols_], cur, cpl[:, cols_].unsqueeze(1).broadcast_to([P, KT, P]), ALU.mult,
                                  after=[c_ok, T.get(("fsumT", s - 1, i))])
                    st.dve(tt, nxt[:, 0, :], cur[:, 0, :], tw[:, 1, cols_], ALU.add, after=[w_ok])
                    ready_ = st.dve(tt, nxt[:, 1, :], cur[:, 1, :], tw[:, 0, cols_], ALU.subtract)
                    cur = nxt
                    yield
                T["cycles", s, i] = c_ok
                f_ok = st.dve(tt, f_sum[:, :, cols_], cur, x2T[:, :, cols_], ALU.add, after=[ready_])
                T["fsum", s, i] = f_ok
                yield
                for k in range(KT):
                    t = st.pe(tr, b.ap[:, k * P:(k + 1) * P], f_sum[:, k, cols_], ident[:, :], after=b.freed + [f_ok])
                T["fsumT", s, i] = t
                n_t, mean, rstd = norm_stats(st, "ffn", [b.ap[:, 0:D]], P, [t], first=i)
                stored = Token(s_out[i2], 16 * (s // 2)) if s >= 2 else None
                t = st.dve(ts, out_sb[:, i2, i, :], b.ap[:, 0:D], mean[0], rstd[0], ALU.subtract, ALU.mult,
                           after=[n_t, stored])
                b.freed = [t]
                T["out", s, i] = t
                yield

            gens = [chain(i, glob() if i == TT - 1 else iter(())) for i in range(TT)]
            for step in zip_longest(*gens[::-1]):
                pass
            ST.sp(nc.sync.dma_start, out[s].rearrange("(i p) d -> p i d", p=P), out_sb[:, i2, :, :], by=16,
                  sem=Token(s_out[i2], 16 * (s // 2 + 1)), after=[T["out", s, i] for i in range(TT)])

        c_cyc = sb("c_cyc", [P, 1])

        mixer_head(0)
        mixer_softplus(0)
        for p in range(NSEQ + 2):
            if p + 1 < NSEQ:
                load_seq(p + 1)
            if p < NSEQ:
                load_ctx(p)
            if p >= 2:
                ffn(p - 2)
            if p < NSEQ:
                mixer_prep(p)
                mixer_front(p)
            if 1 <= p <= NSEQ:
                attn_front(p - 1)
            if p < NSEQ:
                attn_context(p)
                mixer_back(p)
                attn_keys_in(p)
            if 1 <= p <= NSEQ:
                attn_back(p - 1)
            if p + 1 < NSEQ:
                mixer_head(p + 1)
                mixer_softplus(p + 1)
        queues = order(program)

        def play(name, engine):
            passed = {}
            for _, _, after, build, done, by, _, _ in queues[name]:
                need = {}
                for t in after:
                    if t.value > max(passed.get(id(t.sem), 0), need.get(id(t.sem), (0, None))[0]):
                        need[id(t.sem)] = (t.value, t.sem)
                for key, (value, sm) in need.items():
                    engine.wait_ge(sm, value)
                    passed[key] = value
                ins = build()
                if done is not None:
                    ins.then_inc(done.sem, by)

        block = es.enter_context(nc.Block())

        @block.tensor
        def _(e):
            play("pe", e)

        @block.scalar
        def _(e):
            play("act", e)

        @block.vector
        def _(e):
            play("dve", e)

        @block.gpsimd
        def _(e):
            play("pool", e)

        @block.sync
        def _(e):
            play("sp", e)
            for i in range(2):
                n = (NSEQ + 1 - i) // 2
                if n:
                    e.wait_ge(s_out[i], 16 * n)


def kernel(**inputs):
    import numpy as np
    import concourse.bacc as bacc
    from concourse import mybir
    from concourse.bass_utils import run_bass_kernel_spmd as run

    a = {k: np.asarray(v) for k, v in inputs.items()}
    P, DI, NS, H, HD = 128, 512, 16, 8, 64
    f32 = np.float32
    x = np.ascontiguousarray(a["x"])

    w = a["L0_attn_W_in"]
    w_in = np.zeros((w.shape[1], 2 * DI + TAIL), f32)
    w_in[:, 0:DI] = w[DI:2 * DI].T
    w_in[:, DI:2 * DI] = w[0:DI].T
    w_in[:, 2 * DI + ROW_B:2 * DI + ROW_B + NS] = w[2 * DI:2 * DI + NS].T
    w_in[:, 2 * DI + ROW_C:2 * DI + ROW_C + NS] = w[2 * DI + NS:2 * DI + 2 * NS].T
    w_in[:, 2 * DI + ROW_DT:2 * DI + ROW_DT + H] = w[2 * DI + 2 * NS:].T

    cols, n = param_columns()
    par = np.zeros((P, n), f32)
    cw = a["L0_attn_conv_w"][:, 0, :]
    cb = a["L0_attn_conv_b"]
    for c in range(4):
        par[:, cols["conv_w"][0] + 4 * c:cols["conv_w"][0] + 4 * c + 4] = cw[c * P:(c + 1) * P]
        par[:, cols["conv_b"][0] + c] = cb[c * P:(c + 1) * P]
        par[0:HD, cols["D"][0] + c] = a["L0_attn_D"][2 * c]
        par[HD:P, cols["D"][0] + c] = a["L0_attn_D"][2 * c + 1]
        par[:, cols["norm_w"][0] + c] = a["L0_attn_norm_w"][c * P:(c + 1) * P]
    for row, at in ((ROW_B, DI), (ROW_C, DI + NS)):
        par[row:row + NS, cols["conv_w"][0] + 16:cols["conv_w"][0] + 20] = cw[at:at + NS]
        par[row:row + NS, cols["conv_b"][0] + 4] = cb[at:at + NS]
    for name, key in (("ln_m_w", "L0_xattn_ln_m_w"), ("ln_m_b", "L0_xattn_ln_m_b"), ("ln_l_w", "L0_xattn_ln_l_w"),
                      ("ln_l_b", "L0_xattn_ln_l_b"), ("cn_b1", "L0_ffn_cn_b1")):
        par[:, cols[name][0]:cols[name][1]] = a[key].reshape(2, P).T
    par[:, cols["cn_b2"][0]] = a["L0_ffn_cn_b2"]
    par[0:HD, cols["cn_b3"][0]] = a["L0_ffn_cn_b3"]
    par[:, cols["cn_b4"][0]] = a["L0_ffn_cn_b4"][0]
    par[:, cols["gc_b1"][0]] = a["L0_ffn_gc_b1"]
    par[0:HD, cols["gc_b2"][0]] = a["L0_ffn_gc_b2"]
    par[:, cols["gc_b3"][0]] = a["L0_ffn_gc_b3"][0]
    par[:, cols["range"][0]] = a["L0_ffn_adaptive_range"][0]
    par[ROW_DT:ROW_DT + H, cols["dt_bias"][0]] = a["L0_attn_dt_bias"]
    par[ROW_DT:ROW_DT + H, cols["A_log"][0]] = a["L0_attn_A_log"]

    arrays = {
        "x": x, "xT": np.ascontiguousarray(x.transpose(0, 2, 1)), "ctx": a["ctx_1024"], "par": par, "w_in": w_in,
        "w_out": a["L0_attn_W_out"].T, "wq": a["L0_xattn_Wq"], "wkv": a["L0_xattn_Wkv"], "wo": a["L0_xattn_Wout"],
        "cw1": a["L0_ffn_cn_w1"], "cw2": a["L0_ffn_cn_w2"], "cw3": a["L0_ffn_cn_w3"], "cw4": a["L0_ffn_cn_w4"],
        "gw1": a["L0_ffn_gc_w1"], "gw2": a["L0_ffn_gc_w2"], "gw3": a["L0_ffn_gc_w3"],
    }
    arrays = {k: np.ascontiguousarray(v) for k, v in arrays.items()}
    nc = bacc.Bacc("TRN2", target_bir_lowering=False, num_devices=1)
    dram = [nc.dram_tensor(f"in_{k}", v.shape, mybir.dt.float32, kind="ExternalInput").ap() for k, v in arrays.items()]
    result = nc.dram_tensor("result", x.shape, mybir.dt.float32, kind="ExternalOutput").ap()
    decoder_layer(nc, *dram, result)
    r = run(nc, [{f"in_{k}": v for k, v in arrays.items()}], core_ids=[0])
    return r.results[0]["result"]
```

```python
from functools import partial
from itertools import zip_longest


class Token:

    def __init__(self, sem, value):
        self.sem, self.value = sem, value


class Lane:

    def __init__(self, program, stage, engine, sem):
        self.program, self.stage, self.engine, self.sem, self.count = program, stage, engine, sem, 0

    def __call__(self, build, *args, after=(), signal=True, by=1, sem=None, ns=None, table=None, **kw):
        if sem is None and signal:
            self.count += by
            done = Token(self.sem, self.count)
        else:
            done = sem
        self.program.append((self.stage, self.engine, [t for t in after if t], partial(build, *args, **kw),
                             done, by, ns or duration(self.engine, build, args, kw), table))
        return done


class Stage:

    def __init__(self, program, name, sems):
        self.pe, self.act, self.dve, self.pool, self.sp = (
            Lane(program, name, e, s) for e, s in zip(("pe", "act", "dve", "pool", "sp"), sems))


def duration(engine, build, args, kw):
    sizes, pointers, psum = [], 0, False
    for a in list(args) + list(kw.values()):
        if isinstance(a, (int, float, str, bool)) or a is None or "AP" not in type(a).__name__:
            continue
        n = 1
        for d in a.shape[1:]:
            n *= d
        sizes.append(n)
        pointers += n == 1
        psum = psum or a.name.startswith("bank")
    n, name = max(sizes, default=1), build.__name__
    if engine == "pe":
        if name == "transpose":
            return 2 * sizes[0] / 2.4
        passes = 4 if args[1].dtype == args[0].dtype else 1
        half = 0.55 if args[0].shape[0] == 64 and passes == 4 and sizes[0] > 200 else 1
        return 5 + passes * max(sizes[0], 12) / 2.4 * half
    if engine == "act":
        return (50 if psum else 93) + n / 1.2 + (93 if pointers else 0)
    if engine == "dve":
        rate = 1.92 if name in ("tensor_scalar", "tensor_copy") and not psum else 0.96
        return 65 + n / rate + (60 if pointers else 0)
    if engine == "pool":
        return 110 + n * 2.15 if n > 2 else 300 + 164 * n
    return 60


class Bank:

    def __init__(self, ap):
        self.ap, self.freed = ap, []


class Ring:

    def __init__(self, banks):
        self.banks, self.n = banks, 0

    def next(self):
        self.n += 1
        return self.banks[(self.n - 1) % len(self.banks)]


def order(program):
    LATER = {"attn_v": 300, "mixer_decay": 80, "attn_in": 250, "attn": 250}
    SWITCH, OWN = 1300, 50
    HOP = {"pe": 236, "act": 180, "dve": 168, "pool": 96, "sp": 2000}
    lanes, phase_of, left, phase, last = {}, {}, {}, 0, None
    makers, before = {}, []
    for i, (stage, engine, after, _, done, _, _, table) in enumerate(program):
        before.append([makers[id(t.sem), t.value] for t in after])
        lanes.setdefault((engine, stage), []).append(i)
        if table:
            if table != last:
                phase, last = phase + 1, table
            phase_of[i] = phase
            left[phase] = left.get(phase, 0) + 1
        if done is not None:
            makers[id(done.sem), done.value] = i

    at = {k: 0 for k in lanes}
    free = {e: 0.0 for e in ("pe", "act", "dve", "pool", "sp")}
    end, queues, ready, now_phase = {}, {e: [] for e in free}, {}, 1
    for _ in program:
        startable = []
        for key, own in lanes.items():
            if at[key] == len(own):
                continue
            i, engine = own[at[key]], key[0]
            if phase_of.get(i, now_phase) != now_phase:
                continue
            if key not in ready:
                if any(j not in end for j in before[i]):
                    continue
                ready[key] = max([end[j] + (HOP[program[j][1]] if program[j][1] != engine else OWN)
                                  for j in before[i]], default=0.0)
            startable.append((max(free[engine], ready[key]), i + LATER.get(key[1], 0), i, key))
        start, _, i, key = min(startable)
        engine = key[0]
        if i in phase_of:
            left[now_phase] -= 1
            if left[now_phase] == 0:
                now_phase += 1
                free[engine] += SWITCH
        free[engine] = end[i] = max(start, free[engine]) + program[i][6]
        queues[engine].append(program[i])
        at[key] += 1
        del ready[key]
    return queues


def param_columns():
    names = [("conv_w", 20), ("conv_b", 5), ("D", 4), ("norm_w", 4), ("ln_m_w", 2), ("ln_m_b", 2),
             ("ln_l_w", 2), ("ln_l_b", 2), ("cn_b1", 2), ("cn_b2", 1), ("cn_b3", 1), ("cn_b4", 1),
             ("gc_b1", 1), ("gc_b2", 1), ("gc_b3", 1), ("range", 1), ("dt_bias", 1), ("A_log", 1)]
    cols, at = {}, 0
    for n, k in names:
        cols[n] = (at, at + k)
        at += k
    return cols, at


ROW_B, ROW_DT, ROW_C, TAIL = 0, 32, 64, 80


def decoder_layer(nc, x, xT, ctx_in, par_in, w_in, w_out, wq, wkv, wo, cw1, cw2, cw3, cw4, gw1, gw2, gw3, out):
    from contextlib import ExitStack
    from concourse import mybir

    F32, F32R, BF16 = mybir.dt.float32, mybir.dt.float32r, mybir.dt.bfloat16
    ALU, ACT, AX = mybir.AluOpType, mybir.ActivationFunctionType, mybir.AxisListType

    NSEQ, L, D = x.shape
    J = ctx_in.shape[1]
    P = 128
    KT = D // P
    TT = L // P
    H, HD, NS = 8, 64, 16
    DI = H * HD
    CT = DI // P
    NK = J + L
    JT = [(0, J)] + [(J + P * t, P) for t in range(TT)]
    TRI = L + P
    EPS = 1e-5
    MINUS = -1e30
    cols, NPAR = param_columns()
    assert TT == 2 and KT == 2 and TRI == 384

    es = ExitStack()
    with es:
        def sb(name, shape, dt=F32):
            return es.enter_context(nc.sbuf_tensor(name, shape, dt))

        def sem(name):
            return es.enter_context(nc.semaphore(name))

        par = sb("par", [P, NPAR])

        def prm(name, i=0, rows=slice(0, P)):
            a = cols[name][0] + i
            return par[rows, a:a + 1]

        WIN = 2 * DI + TAIL
        w_in_hi, w_in_lo = sb("w_in_hi", [P, KT, WIN], F32R), sb("w_in_lo", [P, KT, WIN], F32R)
        wq_hi, wq_lo = sb("wq_hi", [P, KT, DI], F32R), sb("wq_lo", [P, KT, DI], F32R)
        wkv_hi, wkv_lo = sb("wkv_hi", [P, KT, 2 * DI], F32R), sb("wkv_lo", [P, KT, 2 * DI], F32R)
        w_out_sb, wo_sb = sb("w_out_sb", [P, CT, D]), sb("wo_sb", [P, CT, D])
        cw1_sb, cw2_sb = sb("cw1_sb", [P, KT, D]), sb("cw2_sb", [P, KT, P])
        cw3_sb, cw4_sb = sb("cw3_sb", [P, HD]), sb("cw4_sb", [P, 1])
        cw4_row = sb("cw4_row", [P, P])
        gw1_sb, gw2_sb = sb("gw1_sb", [P, KT, P]), sb("gw2_sb", [P, HD])
        gw3_sb, gw3_row = sb("gw3_sb", [P, 1]), sb("gw3_row", [P, P])
        ident, ones = sb("ident", [P, P]), sb("ones", [P, L])
        ident_b, mask = sb("ident_b", [P, P], BF16), sb("mask", [P, P], BF16)
        pick = sb("pick", [P, H, P], BF16)
        a_neg = sb("a_neg", [P, 1])
        minus_half = sb("minus_half", [P, TT])
        half_b4, half_g3 = sb("half_b4", [P, 1]), sb("half_g3", [P, 1])
        sign = sb("sign", [P, 1])
        tf_gain, gf_gain, c_base = sb("tf_gain", [P, 1]), sb("gf_gain", [P, 1]), sb("c_base", [P, 1])

        xT_sb, x_sb = sb("xT_sb", [P, KT, L]), sb("x_sb", [P, 2, TT, D])
        ctx_sb = sb("ctx_sb", [P, 2, D])
        out_sb = sb("out_sb", [P, TT, D])

        x_hi, x_lo = sb("x_hi", [P, KT, L], F32R), sb("x_lo", [P, KT, L], F32R)
        u, th = sb("u", [P, CT + 1, L]), sb("th", [P, CT + 1, L])
        xc, gate = sb("xc", [P, CT, L]), sb("gate", [P, CT, L])
        Bz, Cz = sb("Bz", [P, L]), sb("Cz", [P, L])
        dt_a, dt_e = sb("dt_a", [P, L]), sb("dt_e", [P, L])
        dc = sb("dc", [P, L])
        c_rest = sb("c_rest", [P, L])
        c_mid, c_parts = sb("c_mid", [P, L], BF16), sb("c_parts", [P, L], BF16)
        ncum, dt_tok = sb("ncum", [P, TT, H]), sb("dt_tok", [P, TT, H])
        G = sb("G", [P, TRI])
        Lm = sb("Lm", [P, H, TRI])
        xdt = sb("xdt", [P, TT, DI])
        g = sb("g", [P, CT, L])
        yD, sq = xc, gate
        ms, rms = sb("ms", [P, TT]), sb("rms", [P, TT])
        x1_pre, x1 = sb("x1_pre", [P, TT, D]), sb("x1", [P, 2, TT, D])

        ctx_n, x1_n = sb("ctx_n", [P, D]), x1_pre
        kv, kv_hi, kv_lo = sb("kv", [P, KT, NK]), sb("kv_hi", [P, KT, NK], F32R), sb("kv_lo", [P, KT, NK], F32R)
        qz_hi, qz_lo = sb("qz_hi", [P, H, L], F32R), sb("qz_lo", [P, H, L], F32R)
        kT_hi, kT_lo = sb("kT_hi", [P, CT, NK], F32R), sb("kT_lo", [P, CT, NK], F32R)
        V = sb("V", [P, len(JT), DI])
        NP = 4
        prob, psum_row, prow_inv = sb("prob", [P, NP, NK]), sb("psum_row", [P, NP]), sb("prow_inv", [P, NP])
        nmax = sb("nmax", [P, NP])
        probT = sb("probT", [P, NP, len(JT), L])
        oT = sb("oT", [P, CT, L])
        x2 = sb("x2", [P, TT, D])
        x2T = sb("x2T", [P, KT, L])
        x2sum = sb("x2sum", [P, KT, TT])

        f_cur = sb("f_cur", [P, KT, L])
        h1, h2, h3 = sb("h1", [P, KT, L]), sb("h2", [P, L]), sb("h3", [P, L])
        t4, cpl, tw = sb("t4", [P, L]), sb("cpl", [P, L]), sb("tw", [P, KT, L])
        g1, g2, tg = sb("g1", [P, 1]), sb("g2", [P, 1]), sb("tg", [P, 1])
        f_sum = tw

        w_raw = Lm[:, :, :].rearrange("p h t -> p (h t)")[:, 0:KT * WIN].rearrange("p (k n) -> p k n", k=KT)
        wkv_raw = probT[:, :, :, :].rearrange("p a j t -> p (a j t)")[:, 0:KT * 2 * DI].rearrange("p (k n) -> p k n", k=KT)
        wq_raw = V[:, :, :].rearrange("p j d -> p (j d)")[:, 0:KT * DI].rearrange("p (k n) -> p k n", k=KT)

        stat = {n: (sb(f"st_{n}", [P, TT, 6]), sb(f"mv_{n}", [P, TT, 2]), sb(f"ve_{n}", [P, TT]),
                    sb(f"rs_{n}", [P, TT])) for n in ("mix", "ctx", "lat", "att", "ffn")}

        banks = [Bank(es.enter_context(nc.psum_tensor(f"bank{i}", [P, 512], F32))) for i in range(8)]
        ring_a, ring_b, ring_c = Ring(banks[0:3]), Ring(banks[3:5]), Ring(banks[5:8])

        program = []

        def stage(name):
            return Stage(program, name, [sem(f"{name}_{e}") for e in ("pe", "act", "dve", "pool", "sp")])

        S = stage("setup")
        I, M, MS, MD, MY = stage("mixer_in"), stage("mixer"), stage("mixer_silu"), stage("mixer_decay"), stage("mixer_y")
        X, XK, XW, XS, XN, XT, XV = (stage("attn"), stage("attn_v"), stage("attn_in"), stage("attn_scores"), stage("attn_norm"), stage("attn_turn"),
                             stage("attn_values"))
        F = [stage(f"ffn{i}") for i in range(TT)]
        LD, ST = stage("load"), stage("store")
        s_par, s_win, s_w = sem("s_par"), sem("s_w_in"), sem("s_w")
        s_x, s_ctx = ([sem(f"{n}{i}") for i in range(2)] for n in ("s_x", "s_ctx"))
        s_out = sem("s_out")
        mm, tr = nc.tensor.matmul, nc.tensor.transpose
        act = nc.scalar.activation
        ts, tt, stt, cp = (nc.vector.tensor_scalar, nc.vector.tensor_tensor,
                           nc.vector.scalar_tensor_tensor, nc.vector.tensor_copy)
        pts, ptt = nc.gpsimd.tensor_scalar, nc.gpsimd.tensor_tensor

        T = {}

        def tok(name, s):
            return T.get((name, s))

        loaded = [0]

        def load_w(dst, src):
            loaded[0] += 16
            return LD.sp(nc.sync.dma_start, dst, src, sem=Token(s_w, loaded[0]), by=16)

        par_in_tok = LD.sp(nc.sync.dma_start, par[:, :], par_in[:, :], sem=Token(s_par, 16), by=16)

        def load_seq(s):
            i, k = s % 2, s // 2 + 1
            LD.sp(nc.sync.dma_start, xT_sb[:, :, :], xT[s].rearrange("(k p) t -> p k t", p=P), by=16,
                  sem=Token(s_x[i], 32 * k - 16), after=[tok("xT_used", s - 1), tok("x_used", s - 2)])
            T["x_in", s] = LD.sp(nc.sync.dma_start, x_sb[:, i, :, :], x[s].rearrange("(k p) d -> p k d", p=P), by=16,
                                 sem=Token(s_x[i], 32 * k))

        def load_ctx(s):
            i, k = s % 2, s // 2 + 1
            T["ctx_in", s] = LD.sp(nc.sync.dma_start, ctx_sb[0:J, i, :], ctx_in[s], by=16, sem=Token(s_ctx[i], 16 * k),
                                   after=[tok("ctx_used", s - 2)])

        w_in_tok = LD.sp(nc.sync.dma_start, w_raw[:, :, :], w_in.rearrange("(k p) n -> p k n", p=P), by=16,
                         sem=Token(s_win, 16))
        load_seq(0)
        for dst, src in ((wq_raw[:, :, :], wq.rearrange("(k p) n -> p k n", p=P)),
                         (wkv_raw[:, :, :], wkv.rearrange("(k p) n -> p k n", p=P)),
                         (w_out_sb[:, :, :], w_out.rearrange("(k p) n -> p k n", p=P)),
                         (wo_sb[:, :, :], wo.rearrange("(k p) n -> p k n", p=P)),
                         (cw1_sb[:, :, :], cw1.rearrange("(k p) n -> p k n", p=P)),
                         (cw2_sb[:, :, :], cw2.rearrange("(k p) n -> p k n", p=P)),
                         (cw3_sb[:, :], cw3), (cw4_sb[0:HD, :], cw4),
                         (gw1_sb[:, :, :], gw1.rearrange("(k p) n -> p k n", p=P)),
                         (gw2_sb[:, :], gw2), (gw3_sb[0:HD, :], gw3)):
            w_tok = load_w(dst, src)

        pd, dv = S.pool, S.dve

        def split(raw, hi, lo, t):
            for k in range(KT):
                h_ok = dv(cp, hi[:, k, :], raw[:, k, :], after=[t])
                l_ok = dv(tt, lo[:, k, :], raw[:, k, :], hi[:, k, :].bitcast(F32), ALU.subtract, after=[h_ok])
            return l_ok

        a0, a1 = cols["conv_w"][0], cols["conv_b"][1]
        dv(nc.vector.memset, ones[:, :], 1.0)
        dv(nc.vector.memset, minus_half[:, :], -0.5)
        dv(nc.vector.memset, sign[0:64, :], 1.0)
        dv(nc.vector.memset, sign[64:P, :], -1.0)
        for b in banks:
            zeros = dv(nc.vector.memset, b.ap[:, :], 0.0)
        for b in (Bz, Cz, dc, g2):
            dv(nc.vector.memset, b[:, :], 0.0)
        dv(nc.vector.memset, c_parts[:, :], 0.0)
        dv(ts, par[:, a0:a1], par[:, a0:a1], 0.5, None, ALU.mult, after=[par_in_tok])
        dv(ts, half_b4[:, :], prm("cn_b4"), 0.5, None, ALU.mult)
        dv(ts, half_g3[:, :], prm("gc_b3"), 0.5, None, ALU.mult)
        dv(ts, tf_gain[:, :], prm("range"), sign[:, :], 0.3, ALU.mult, ALU.mult, after=[zeros])
        dv(ts, gf_gain[:, :], prm("range"), sign[:, :], 0.7, ALU.mult, ALU.mult)
        dv(ts, c_base[:, :], sign[:, :], 0.1, None, ALU.mult)
        ea = S.act(act, a_neg[ROW_DT:ROW_DT + H, :], prm("A_log", 0, slice(ROW_DT, ROW_DT + H)), ACT.Exp, table="exp",
                   after=[par_in_tok])
        dv(ts, a_neg[ROW_DT:ROW_DT + H, :], a_neg[ROW_DT:ROW_DT + H, :], -1.0, None, ALU.mult, after=[ea])
        win = dv(ts, w_raw[:, :, DI:2 * DI], w_raw[:, :, DI:2 * DI], 0.5, None, ALU.mult, after=[w_in_tok])
        w_in_ok = split(w_raw, w_in_hi, w_in_lo, win)

        z_id = pd(nc.gpsimd.memset, ident[:, :], 0.0)
        z_ca = pd(nc.gpsimd.memset, mask[:, :], 0.0)
        z_pk = pd(nc.gpsimd.memset, pick[:, :, :], 0.0)
        id_ok = pd(nc.gpsimd.affine_select, out=ident[:, :], in_=ident[:, :], compare_op=ALU.not_equal, fill=1.0,
                   base=0, pattern=[[-1, P]], channel_multiplier=1, after=[z_id])
        ib_ok = pd(nc.gpsimd.tensor_copy, ident_b[:, :], ident[:, :], after=[id_ok])
        z_ca = pd(nc.gpsimd.affine_select, out=mask[:, :], in_=mask[:, :], compare_op=ALU.is_ge, fill=MINUS, base=0,
                  pattern=[[1, P]], channel_multiplier=-1, after=[z_ca])
        for r0 in (0, 32, 64):
            z_pk = pd(nc.gpsimd.affine_select, out=pick[:, :, :], in_=pick[:, :, :], compare_op=ALU.not_equal,
                      fill=1.0, base=-r0, pattern=[[-1, H], [0, P]], channel_multiplier=1, after=[z_pk])
        for b in (qz_hi, qz_lo):
            qz_ok = pd(nc.gpsimd.memset, b[:, :, :].bitcast(F32), 0.0)
        T["setup_mixer"] = [w_in_ok, ib_ok, z_ca, z_pk]

        for b in (h3, gw3_row, cw4_row):
            zeros = dv(nc.vector.memset, b[:, :], 0.0)
        for k in range(CT):
            dv(ts, w_out_sb[:, k, :], w_out_sb[:, k, :], prm("norm_w", k), None, ALU.mult, after=[w_tok])
        wq_ok = dv(ts, wq_raw[:, :, :], wq_raw[:, :, :], float(HD) ** -0.5, None, ALU.mult)
        wq_ok = split(wq_raw, wq_hi, wq_lo, wq_ok)
        split(wkv_raw, wkv_hi, wkv_lo, None)
        dv(ts, cw4_row[0:HD, :], ones[0:HD, 0:P], cw4_sb[0:HD, :], None, ALU.mult, after=[zeros])
        T["setup"] = [dv(ts, gw3_row[0:HD, :], ones[0:HD, 0:P], gw3_sb[0:HD, :], None, ALU.mult), qz_ok]

        def norm_stats(st, name, src, rows, after, first=0):
            stats, mv, ve, rs = stat[name]
            tiles = range(first, first + len(src))
            c = slice(first, first + len(src))
            for i, a in zip(tiles, src):
                t = st.dve(nc.vector.bn_stats, stats[0:rows, i, :], a, after=after)
            for i in tiles:
                t = st.dve(nc.vector.bn_aggr, mv[0:rows, i, :], stats[0:rows, i, :], after=[t])
            t = st.pool(pts, ve[0:rows, c], mv[0:rows, c, 1], EPS, None, ALU.add, after=[t])
            t = st.pool(ptt, rs[0:rows, c], ve[0:rows, c], minus_half[0:rows, c], ALU.pow, after=[t])
            return t, [mv[0:rows, i, 0:1] for i in tiles], [rs[0:rows, i:i + 1] for i in tiles]

        def product3(st, dst, w_hi, w_lo, x_hi_, x_lo_, after, x_is_rhs=True):
            n = 0
            for k in range(KT):
                for w_, x_ in ((w_hi[k], x_hi_[k]), (w_lo[k], x_hi_[k]), (w_hi[k], x_lo_[k])):
                    a, b = (w_, x_) if x_is_rhs else (x_, w_)
                    n += 1
                    t = st.pe(mm, dst, a, b, start=n == 1, stop=n == 3 * KT, signal=n == 3 * KT,
                              after=after if n == 1 else ())
            return t

        def project(dst, c0, n, after):
            return product3(I, dst, [w_in_hi[:, k, c0:c0 + n] for k in range(KT)],
                            [w_in_lo[:, k, c0:c0 + n] for k in range(KT)],
                            [x_hi[:, k, :] for k in range(KT)], [x_lo[:, k, :] for k in range(KT)], after)

        def conv(s, src, c, rows, ready_):
            return I.act(act, u[0:rows, c, :], src, ACT.Identity, scale=prm("conv_w", 4 * c + 3, slice(0, rows)),
                         bias=prm("conv_b", c, slice(0, rows)), after=[ready_, tok("conv", s - 1)])

        def taps(src, c, rows, after):
            for d in (1, 2, 3):
                after = [I.dve(stt, u[0:rows, c, d:L], src[:, 0:L - d], prm("conv_w", 4 * c + 3 - d, slice(0, rows)),
                               u[0:rows, c, d:L], ALU.mult, ALU.add, after=after)]
            return after[0]

        def mixer_head(s):
            i = s % 2
            hi_ok = I.act(act, x_hi[:, :, :], xT_sb[:, :, :], ACT.Copy,
                          after=[tok("x_in", s), tok("in_proj", s - 1)])
            lo_ok = I.dve(tt, x_lo[:, :, :], xT_sb[:, :, :], x_hi[:, :, :].bitcast(F32), ALU.subtract, after=[hi_ok])
            T["xT_used", s] = lo_ok
            T["x_split", s] = [hi_ok, lo_ok]

            b = ring_c.next()
            p_ok = project(b.ap[0:TAIL, 0:L], 2 * DI, TAIL, b.freed + T["setup_mixer"] + [hi_ok, lo_ok])
            c_ok = conv(s, b.ap[0:TAIL, 0:L], CT, TAIL, p_ok)
            u_ok = taps(b.ap[0:TAIL, 0:L], CT, TAIL, [c_ok])
            a_ok = I.dve(ts, dt_a[ROW_DT:ROW_DT + H, :], b.ap[ROW_DT:ROW_DT + H, 0:L],
                         prm("dt_bias", 0, slice(ROW_DT, ROW_DT + H)), None, ALU.add,
                         after=[p_ok, tok("dt", s - 1)])
            T["dt_a", s] = a_ok
            b.freed = [a_ok]
            t_ok = MS.act(act, th[0:TAIL, CT, :], u[0:TAIL, CT, :], ACT.Tanh, after=[u_ok, tok("BC", s - 1)])
            MS.dve(stt, Bz[0:NS, :], th[0:NS, CT, :], 1.0, u[0:NS, CT, :], ALU.add, ALU.mult,
                  after=[t_ok, tok("CB", s - 1)])
            T["BC", s] = MS.dve(stt, Cz[0:NS, :], th[ROW_C:ROW_C + NS, CT, :], 1.0, u[ROW_C:ROW_C + NS, CT, :],
                               ALU.add, ALU.mult)

        def mixer_front(s):
            for j in range(CT // 2):
                b = ring_c.next()
                aps = [b.ap[:, 0:L], b.ap[:, L:2 * L]]
                after = b.freed + T["x_split", s]
                for e in range(2):
                    p_ok = project(aps[e], (2 * j + e) * P, P, after)
                    after = []
                c_ok = [conv(s, aps[e], 2 * j + e, P, p_ok) for e in range(2)]
                u_ok = [taps(aps[e], 2 * j + e, P, c_ok) for e in range(2)]
                b.freed = [u_ok[1]]
                t_ok = MS.act(act, th[:, 2 * j:2 * j + 2, :], u[:, 2 * j:2 * j + 2, :], ACT.Tanh, after=u_ok + [tok("gate", s - 1)])
                T["xc", s] = MS.dve(stt, xc[:, 2 * j:2 * j + 2, :], th[:, 2 * j:2 * j + 2, :], 1.0,
                                   u[:, 2 * j:2 * j + 2, :], ALU.add, ALU.mult, after=[t_ok, tok("xc_used", s - 1)])
            T["conv", s] = T["xc", s]
            for j in range(CT // 2):
                b = ring_c.next()
                after = b.freed
                for e in range(2):
                    p_ok = project(b.ap[:, e * L:(e + 1) * L], DI + (2 * j + e) * P, P, after)
                    after = []
                flat = b.ap[:, :].rearrange("p (e t) -> p e t", e=2)
                t_ok = MS.act(act, th[:, 2 * j:2 * j + 2, :], flat, ACT.Tanh, after=[p_ok, T["xc", s]])
                g_ok = MS.dve(stt, gate[:, 2 * j:2 * j + 2, :], th[:, 2 * j:2 * j + 2, :], 1.0, flat, ALU.add, ALU.mult,
                             after=[t_ok, tok("ms", s - 1)])
                b.freed = [g_ok]
            T["gate", s] = g_ok
            T["in_proj", s] = p_ok

        def mixer_softplus(s):
            r = slice(ROW_DT, ROW_DT + H)
            n_ok = M.dve(stt, dt_e[r, :], dt_a[r, :], -1.0, dt_a[r, :], ALU.mult, ALU.min, after=[T["dt_a", s]])
            e_ok = M.act(act, dt_e[r, :], dt_e[r, :], ACT.Exp, table="exp", after=[n_ok])
            l_ok = M.act(act, dt_e[r, :], dt_e[r, :], ACT.Ln, table="ln", bias=ones[r, 0:1], after=[e_ok])
            T["ln", s] = l_ok

        def mixer_prep(s):
            r = slice(ROW_DT, ROW_DT + H)
            d_ok = M.dve(stt, dc[r, :], dt_a[r, :], 0.0, dt_e[r, :], ALU.max, ALU.add,
                         after=[T["ln", s], tok("dc_used", s - 1)])
            T["dt", s] = d_ok
            a_ok = M.dve(ts, dt_e[r, :], dc[r, :], a_neg[r, :], None, ALU.mult, after=[d_ok])
            c_ok = M.dve(nc.vector.tensor_tensor_scan, dc[0:H, :], ones[r, :], dt_e[r, :], 0.0, ALU.mult, ALU.add,
                         after=[a_ok])
            t = M.pool(pts, c_parts[0:H, :], dc[0:H, :], 1.0, None, ALU.mult, after=[c_ok, tok("parts_used", s - 1)])
            t = M.pool(ptt, c_rest[0:H, :], dc[0:H, :], c_parts[0:H, :], ALU.subtract, after=[t])
            t = M.pool(pts, c_mid[0:H, :], c_rest[0:H, :], 1.0, None, ALU.mult, after=[t])
            M.dve(cp, c_parts[32:32 + H, :], c_rest[0:H, :], after=[t])
            T["parts", s] = M.dve(tt, c_parts[64:64 + H, :], c_rest[0:H, :], c_mid[0:H, :], ALU.subtract)
            T["cum", s] = c_ok

            b = ring_c.next()
            for i in range(TT):
                t = M.pe(tr, b.ap[:, i * 64:i * 64 + 40], dc[0:40, i * P:(i + 1) * P], ident[0:40, 0:40],
                         after=b.freed + [T["cum", s]])
            T["dc_used", s] = t
            bt = b.ap[:, 0:64 * TT].rearrange("p (i c) -> p i c", i=TT)
            n_ok = M.dve(ts, ncum[:, :, :], bt[:, :, 0:H], -1.0, None, ALU.mult, after=[t, tok("decay_all", s - 1)])
            d_ok = M.dve(cp, dt_tok[:, :, :], bt[:, :, 32:32 + H], after=[tok("xdt", s - 1)])
            b.freed = [d_ok]

            b = ring_c.next()
            M.pe(mm, b.ap[:, 0:L], Bz[:, 0:P], Cz[:, :], start=True, stop=True, after=b.freed + [T["BC", s]], signal=False)
            t = M.pe(mm, b.ap[:, L:TRI], Bz[:, P:L], Cz[:, P:L], start=True, stop=True)
            T["CB", s] = t
            G_ok = M.act(act, G[:, :], b.ap[:, 0:TRI], ACT.Copy, after=[t, tok("Lm", s - 1)])
            b.freed = [G_ok]

            T["G", s], T["dt_tok", s] = G_ok, d_ok
            T["ncum", s] = n_ok

        def mixer_back(s):
            for i in range(TT):
                b = ring_c.next()
                for c in range(CT):
                    t = M.pe(tr, b.ap[:, c * P:(c + 1) * P], xc[:, c, i * P:(i + 1) * P], ident[:, :], signal=c == CT - 1,
                             after=b.freed + [T["xc", s]] if c == 0 else ())
                xdt_ok = M.dve(tt, xdt[:, i, :].rearrange("p (h d) -> p h d", h=H), b.ap[:, :].rearrange("p (h d) -> p h d", h=H),
                               dt_tok[:, i, :].unsqueeze(2).broadcast_to([P, H, HD]), ALU.mult,
                               after=[t, T["dt_tok", s], tok("y", s - 1)])
                b.freed = [xdt_ok]
            T["xdt", s] = xdt_ok

            def decay(q):
                for h in (2 * q, 2 * q + 1):
                    b = ring_c.next()
                    for c0, m0, m1 in ((0, 0, L), (P, L, TRI)):
                        MD.pe(mm, b.ap[:, m0:m1], pick[:, h, :], c_parts[:, c0:L], start=True, stop=False, signal=False,
                              after=b.freed + [T["parts", s]])
                        t = MD.pe(mm, b.ap[:, m0:m0 + P], ident_b[:, :], mask[:, :], start=False, stop=True,
                                  signal=m0 > 0)
                    T["parts_used", s] = t
                    for i, m0, m1 in ((0, 0, L), (1, L, TRI)):
                        e_ok = MD.act(act, Lm[:, h, m0:m1], b.ap[:, m0:m1], ACT.Exp, table="exp", bias=ncum[:, i, h:h + 1],
                                      after=[t, T["ncum", s], tok("y", s - 1)])
                    b.freed = [e_ok]
                T["decay_all", s] = e_ok
                pair = Lm[:, 2 * q:2 * q + 2, :]
                return MD.pool(ptt, pair, pair, G[:, :].unsqueeze(1).broadcast_to([P, 2, TRI]), ALU.mult,
                               after=[e_ok, T["G", s]])

            def y_pair(q, lm_ok):
                b = ring_c.next()
                for i, (c0, c1, m0) in enumerate(((0, L, 0), (P, L, L))):
                    for e in range(2):
                        h = 2 * q + e
                        t = MY.pe(mm, b.ap[e * HD:(e + 1) * HD, c0:c1], xdt[:, i, h * HD:(h + 1) * HD],
                                 Lm[:, h, m0:m0 + c1 - c0], start=i == 0, stop=i == 1, signal=i == 1 and e == 1,
                                 after=b.freed + [lm_ok, xdt_ok] if i == 0 and e == 0 else ())
                T["y", s] = t
                y_ok = MY.dve(stt, yD[:, q, :], xc[:, q, :], prm("D", q), b.ap[:, 0:L], ALU.mult, ALU.add,
                             after=[t])
                b.freed = [y_ok]
                g_ok = MY.pool(ptt, g[:, q, :], yD[:, q, :], gate[:, q, :], ALU.mult,
                              after=[y_ok, tok("gate", s), tok("out_proj", s - 1)])
                T["xc_used", s] = g_ok
                return g_ok, MY.act(act, sq[:, q, :], g[:, q, :], ACT.Square, after=[g_ok, tok("gate", s)])

            lm_ok = {}
            for q in range(CT + 2):
                if q < CT:
                    T["Lm", s] = lm_ok[q] = decay(q)
                if q > 1:
                    g_ok, sq_ok = y_pair(q - 2, lm_ok[q - 2])

            t = M.pool(ptt, sq[:, 0:2, :], sq[:, 0:2, :], sq[:, 2:4, :], ALU.add, after=[sq_ok])
            t = M.pool(ptt, sq[:, 0, :], sq[:, 0, :], sq[:, 1, :], ALU.add, after=[t])
            b2 = ring_c.next()
            for i in range(TT):
                for c in range(CT):
                    o_ok = M.pe(mm, b2.ap[:, i * D:(i + 1) * D], g[:, c, i * P:(i + 1) * P], w_out_sb[:, c, :],
                                start=c == 0, stop=c == CT - 1, signal=c == CT - 1,
                                after=b2.freed + [g_ok] + T["setup"] if i == 0 and c == 0 else ())
            T["out_proj", s] = o_ok
            b = ring_c.next()
            for i in range(TT):
                m_ok = M.pe(mm, b.ap[:, 2 * i:2 * i + 2], sq[:, 0, i * P:(i + 1) * P], ones[:, 0:2], start=True, stop=True,
                            after=b.freed + [t])
            v_ok = M.dve(ts, ms[:, :], b.ap[:, 0:2 * TT].rearrange("p (i c) -> p i c", c=2)[:, :, 0], 1.0 / DI, EPS,
                         ALU.mult, ALU.add, after=[m_ok, tok("rms", s - 1)])
            b.freed = [v_ok]
            T["ms", s] = m_ok
            r_ok = M.pool(ptt, rms[:, :], ms[:, :], minus_half[:, :], ALU.pow, after=[v_ok, tok("x_used", s - 1)])
            T["rms", s] = r_ok
            for i in range(TT):
                t = M.dve(stt, x1_pre[:, i, :], b2.ap[:, i * D:(i + 1) * D], rms[:, i:i + 1], x_sb[:, s % 2, i, :],
                          ALU.mult, ALU.add, after=[r_ok, o_ok, tok("x1T", s - 1)])
            b2.freed = [t]
            T["x_used", s] = t
            n_t, mean, rstd = norm_stats(M, "mix", [x1_pre[:, i, :] for i in range(TT)], P, [t])
            for i in range(TT):
                t = M.dve(ts, x1[:, s % 2, i, :], x1_pre[:, i, :], mean[i], rstd[i], ALU.subtract, ALU.mult,
                          after=[n_t, tok("x1_used", s - 2)])
            T["x1", s] = t
            n_t, mean, rstd = norm_stats(M, "lat", [x1[:, s % 2, i, :] for i in range(TT)], P, [T["x1", s]])
            for i in range(TT):
                t = M.dve(ts, x1_n[:, i, :], x1[:, s % 2, i, :], mean[i], rstd[i], ALU.subtract, ALU.mult,
                          after=[n_t, tok("x1T", s - 1)])
            T["x1_n", s] = t

        def attn_context(s):
            i2 = s % 2
            n_t, mean, rstd = norm_stats(XK, "ctx", [ctx_sb[0:J, i2, :]], J, [tok("ctx_in", s)])
            t = XK.dve(ts, ctx_n[0:J, :], ctx_sb[0:J, i2, :], mean[0], rstd[0], ALU.subtract, ALU.mult,
                      after=[n_t, tok("ctxT", s - 1)])
            T["ctx_used", s] = t
            b = ring_c.next()
            for k in range(KT):
                c_ok = XK.pe(tr, b.ap[:, k * J:(k + 1) * J], ctx_n[0:J, k * P:(k + 1) * P], ident[0:J, 0:J],
                            after=b.freed + [t] + T["setup_mixer"])
            T["ctxT", s] = c_ok
            for k in range(KT):
                kv_c = XK.act(act, kv[:, k, 0:J], b.ap[:, k * J:(k + 1) * J], ACT.Identity, scale=prm("ln_m_w", k),
                             bias=prm("ln_m_b", k), after=[c_ok, tok("kv_used", s - 1)])
            b.freed = [kv_c]
            T["kv_c", s] = kv_c

        def attn_keys_in(s):
            b = ring_c.next()
            for k in range(KT):
                for i in range(TT):
                    l_ok = XK.pe(tr, b.ap[:, k * L + i * P:k * L + (i + 1) * P], x1_n[:, i, k * P:(k + 1) * P], ident[:, :],
                                after=b.freed + [T["x1_n", s]])
            T["x1T", s] = l_ok
            for k in range(KT):
                kv_l = XK.act(act, kv[:, k, J:NK], b.ap[:, k * L:(k + 1) * L], ACT.Identity, scale=prm("ln_l_w", k),
                             bias=prm("ln_l_b", k), after=[l_ok])
            b.freed = [kv_l]
            hi_ok = XK.dve(cp, kv_hi[:, :, :], kv[:, :, :], after=[kv_l, T["kv_c", s], tok("proj", s - 1)])
            lo_ok = XK.dve(tt, kv_lo[:, :, :], kv[:, :, :], kv_hi[:, :, :].bitcast(F32), ALU.subtract, after=[hi_ok])
            T["kv_used", s] = lo_ok
            T["kv", s] = [hi_ok, lo_ok]

        def attn_front(s):
            i2 = s % 2
            x_ok = T["kv", s] + T["setup"]

            def q_pair(j):
                b = ring_b.next()
                after = b.freed + x_ok
                for e in range(2):
                    c0 = (2 * j + e) * P
                    p_ok = product3(X, b.ap[:, e * L:(e + 1) * L], [wq_hi[:, k, c0:c0 + P] for k in range(KT)],
                                    [wq_lo[:, k, c0:c0 + P] for k in range(KT)], [kv_hi[:, k, J:NK] for k in range(KT)],
                                    [kv_lo[:, k, J:NK] for k in range(KT)], after)
                    after = []
                T["qz", s, j] = []
                for e in range(2):
                    r = slice(e * HD, (e + 1) * HD)
                    hi, lo = (q[r, 4 * j:4 * j + 4, :].rearrange("p (c e) t -> p c e t", e=2)[:, :, e, :] for q in (qz_hi, qz_lo))
                    src = b.ap[r, :].rearrange("p (c t) -> p c t", c=2)
                    hi_ok = X.act(act, hi, src, ACT.Copy, after=[p_ok, tok("scores", s - 1)] + T["setup"])
                    lo_ok = X.dve(tt, lo, src, hi.bitcast(F32), ALU.subtract, after=[hi_ok])
                    T["qz", s, j] += [hi_ok, lo_ok]
                b.freed = [lo_ok]

            def k_tile(c):
                b = ring_b.next()
                p_ok = product3(X, b.ap[:, 0:NK], [wkv_hi[:, k, c * P:(c + 1) * P] for k in range(KT)],
                                [wkv_lo[:, k, c * P:(c + 1) * P] for k in range(KT)], [kv_hi[:, k, :] for k in range(KT)],
                                [kv_lo[:, k, :] for k in range(KT)], b.freed + x_ok)
                hi_ok = X.act(act, kT_hi[:, c, :], b.ap[:, 0:NK], ACT.Copy, after=[p_ok, tok("scores", s - 1)])
                lo_ok = X.dve(tt, kT_lo[:, c, :], b.ap[:, 0:NK], kT_hi[:, c, :].bitcast(F32), ALU.subtract, after=[hi_ok])
                b.freed = [lo_ok]
                T["kT", s, c] = [hi_ok, lo_ok]

            def v_tile(j):
                j0, n = JT[j]
                b = ring_b.next()
                p_ok = product3(XW, b.ap[0:n, :], [wkv_hi[:, k, DI:2 * DI] for k in range(KT)],
                                [wkv_lo[:, k, DI:2 * DI] for k in range(KT)], [kv_hi[:, k, j0:j0 + n] for k in range(KT)],
                                [kv_lo[:, k, j0:j0 + n] for k in range(KT)], b.freed + x_ok, x_is_rhs=False)
                t = XW.act(act, V[0:n, j, :], b.ap[0:n, :], ACT.Copy, after=[p_ok, tok("attn", s - 1)])
                b.freed = [t]
                T["V", s] = t
                T["proj", s] = p_ok

            for j in range(CT // 2):
                q_pair(j)
            for c in range(CT):
                k_tile(c)
            for j in range(len(JT)):
                v_tile(j)

        def attn_back(s):
            NU, LAG = H * TT, 3
            p_ok, pt_ok, o_ok = {}, {}, None

            def scores(n):
                h, i, r = n // TT, n % TT, n % NP
                b = ring_a.next()
                for k, (q_, k_) in enumerate(((qz_hi, kT_hi), (qz_lo, kT_hi), (qz_hi, kT_lo))):
                    t = XS.pe(mm, b.ap[:, 0:NK], q_[:, h, i * P:(i + 1) * P], k_[:, h // 2, :], start=k == 0, stop=k == 2,
                              signal=k == 2, after=b.freed + T["qz", s, h // 4] + T["kT", s, h // 2] if k == 0 else ())
                T["scores", s] = t
                m_ok = XS.dve(nc.vector.tensor_reduce, nmax[:, r:r + 1], b.ap[:, 0:NK], AX.X, ALU.max, negate=True,
                             after=[t, T.get("exp", {}).get(r)])
                e_ok = XS.act(act, prob[:, r, :], b.ap[:, 0:NK], ACT.Exp, table="exp", bias=nmax[:, r:r + 1],
                             accum_out=psum_row[:, r:r + 1], after=[m_ok, T.get("prob_used", {}).get(r)])
                T.setdefault("exp", {})[r] = e_ok
                b.freed = [e_ok]
                i_ok = XN.dve(nc.vector.reciprocal, prow_inv[:, r:r + 1], psum_row[:, r:r + 1],
                             after=[e_ok, T.get("inv_used", {}).get(r)])
                p_ok[n] = XN.dve(ts, prob[:, r, :], prob[:, r, :], prow_inv[:, r:r + 1], None, ALU.mult, after=[i_ok])
                T.setdefault("inv_used", {})[r] = p_ok[n]

            def turn(n):
                h, i, r = n // TT, n % TT, n % NP
                b = ring_b.next()
                for j, (j0, m) in enumerate(JT):
                    t = XT.pe(tr, b.ap[0:m, j * P:(j + 1) * P], prob[:, r, j0:j0 + m], ident[:, :],
                             signal=j == len(JT) - 1, after=b.freed + [p_ok[n]] if j == 0 else ())
                T.setdefault("prob_used", {})[r] = t
                src = b.ap[:, 0:len(JT) * P].rearrange("p (j i) -> p j i", j=len(JT))
                dst = probT[:, h % NP, :, i * P:(i + 1) * P]
                after = [t, T.get("probT_used", {}).get(h % NP)]
                pt_ok[n] = XT.act(act, dst, src, ACT.Copy, after=after) if n % 2 else XT.dve(cp, dst, src, after=after)
                b.freed = [pt_ok[n]]

            def values(q):
                b = ring_b.next()
                for j, (_, m) in enumerate(JT):
                    for e in range(2):
                        h = 2 * q + e
                        t = XV.pe(mm, b.ap[e * HD:(e + 1) * HD, 0:L], V[0:m, j, h * HD:(h + 1) * HD],
                                 probT[0:m, h % NP, j, :], start=j == 0, stop=j == len(JT) - 1,
                                 signal=j == len(JT) - 1 and e == 1,
                                 after=b.freed + [T["V", s]] + [pt_ok[n] for n in range(4 * q, 4 * q + 4)]
                                 if j == 0 and e == 0 else ())
                for e in range(2):
                    T.setdefault("probT_used", {})[(2 * q + e) % NP] = t
                T["attn", s] = t
                t = XV.act(act, oT[:, q, :], b.ap[:, 0:L], ACT.Copy, after=[t, tok("wo", s - 1)])
                b.freed = [t]
                return t

            for n in range(NU + LAG + 2):
                if n < NU:
                    scores(n)
                if 0 <= n - LAG < NU:
                    turn(n - LAG)
                if n - LAG - 1 >= 0 and (n - LAG - 1) % 4 == 3:
                    o_ok = values((n - LAG - 1) // 4)

            for i in range(TT):
                b = ring_b.next()
                for c in range(CT):
                    t = XV.pe(mm, b.ap[:, 0:D], oT[:, c, i * P:(i + 1) * P], wo_sb[:, c, :], start=c == 0,
                             stop=c == CT - 1, signal=c == CT - 1, after=b.freed + [o_ok] if c == 0 else ())
                T["x2_pre", s, i] = XV.dve(tt, x2[:, i, :], b.ap[:, 0:D], x1[:, s % 2, i, :], ALU.add,
                                           after=[t, T.get(("x2T_pe", s - 1, i))])
                b.freed = [T["x2_pre", s, i]]
            T["wo", s] = t
            T["x1_used", s] = T["x2_pre", s, TT - 1]


        def ffn(s):
            i2 = s % 2
            x2T_ok, base = {}, {}

            def glob():
                st, b = F[TT - 1], banks[TT - 1]
                for k in range(KT):
                    for i in range(TT):
                        t = st.pe(mm, b.ap[:, 0:1], gw1_sb[:, k, :], x2sum[:, k, i:i + 1], start=k + i == 0,
                                  stop=k + i == KT + TT - 2, signal=k + i == KT + TT - 2,
                                  after=b.freed + [x2T_ok[n] for n in range(TT)])
                T["x2sum_used", s] = t
                t = st.act(act, g1[:, :], b.ap[:, 0:1], ACT.Gelu, table="gelu", bias=prm("gc_b1"), scale=1.0 / L,
                           after=[t, tok("g1_used", s - 1)])
                b.freed = [t]
                yield
                t = st.pe(mm, b.ap[0:HD, 0:1], gw2_sb[:, :], g1[:, :], start=True, stop=True, after=b.freed + [t])
                T["g1_used", s] = t
                t = st.act(act, g2[0:HD, :], b.ap[0:HD, 0:1], ACT.Gelu, table="gelu", bias=prm("gc_b2", 0, slice(0, HD)),
                           after=[t, tok("g2_used", s - 1)])
                b.freed = [t]
                yield
                t = st.pe(mm, b.ap[:, 0:1], gw3_row[:, :], g2[:, :], start=True, stop=True, after=b.freed + [t])
                T["g2_used", s] = t
                t = st.act(act, tg[:, :], b.ap[:, 0:1], ACT.Tanh, bias=half_g3[:, :], scale=0.5, after=[t, tok("base", s - 1)])
                b.freed = [t]
                T["base", s] = st.dve(stt, c_cyc[:, :], tg[:, :], gf_gain[:, :], c_base[:, :], ALU.mult, ALU.add,
                                      after=[t] + [T.get(("cycles", s - 1, n)) for n in range(TT)])
                yield

            def chain(i, gen):
                st, b = F[i], banks[i]
                cols_ = slice(i * P, (i + 1) * P)
                n_t, mean, rstd = norm_stats(st, "att", [x2[:, i, :]], P, [T["x2_pre", s, i]], first=i)
                t = st.dve(ts, x2[:, i, :], x2[:, i, :], mean[0], rstd[0], ALU.subtract, ALU.mult, after=[n_t])
                yield
                for k in range(KT):
                    t_ok = st.pe(tr, b.ap[:, k * P:(k + 1) * P], x2[:, i, k * P:(k + 1) * P], ident[:, :],
                                 after=b.freed + [t])
                T["x2T_pe", s, i] = t_ok
                for k in range(KT):
                    t = st.act(act, x2T[:, k, cols_], b.ap[:, k * P:(k + 1) * P], ACT.Copy,
                               accum_out=x2sum[:, k, i:i + 1],
                               after=[t_ok, T.get(("fsum", s - 1, i)), tok("x2sum_used", s - 1)])
                b.freed = [t]
                x2T_ok[i] = ready_ = t
                yield
                cur, nxt = x2T[:, :, cols_], f_cur[:, :, cols_]
                for cyc in range(3):
                    for m in range(KT):
                        for k in range(KT):
                            t = st.pe(mm, b.ap[:, m * P:(m + 1) * P], cw1_sb[:, k, m * P:(m + 1) * P], cur[:, k, :],
                                      start=k == 0, stop=k == KT - 1, signal=k == KT - 1,
                                      after=b.freed + [ready_] if m == 0 and k == 0 else ())
                    for m in range(KT):
                        a = st.act(act, h1[:, m, cols_], b.ap[:, m * P:(m + 1) * P], ACT.Gelu, table="gelu",
                                   bias=prm("cn_b1", m), after=[t])
                    b.freed = [a]
                    yield
                    for _ in zip(gen, (0,)) if cyc == 0 else ():
                        pass
                    for k in range(KT):
                        t = st.pe(mm, b.ap[:, 0:P], cw2_sb[:, k, :], h1[:, k, cols_], start=k == 0, stop=k == KT - 1,
                                  signal=k == KT - 1, after=b.freed + [a] if k == 0 else ())
                    a = st.act(act, h2[:, cols_], b.ap[:, 0:P], ACT.Gelu, table="gelu", bias=prm("cn_b2"), after=[t])
                    b.freed = [a]
                    yield
                    for _ in zip(gen, (0,)) if cyc == 0 else ():
                        pass
                    t = st.pe(mm, b.ap[0:HD, 0:P], cw3_sb[:, :], h2[:, cols_], start=True, stop=True, after=b.freed + [a])
                    a = st.act(act, h3[0:HD, cols_], b.ap[0:HD, 0:P], ACT.Gelu, table="gelu",
                               bias=prm("cn_b3", 0, slice(0, HD)), after=[t])
                    b.freed = [a]
                    yield
                    for _ in gen if cyc == 0 else ():
                        pass
                    t = st.pe(mm, b.ap[:, 0:P], cw4_row[:, :], h3[:, cols_], start=True, stop=True, after=b.freed + [a])
                    a = st.act(act, t4[:, cols_], b.ap[:, 0:P], ACT.Tanh, bias=half_b4[:, :], scale=0.5, after=[t])
                    b.freed = [a]
                    yield
                    c_ok = st.dve(ts, cpl[:, cols_], t4[:, cols_], tf_gain[:, :], c_cyc[:, :], ALU.mult, ALU.add,
                                  after=[a, T["base", s]])
                    w_ok = st.dve(tt, tw[:, :, cols_], cur, cpl[:, cols_].unsqueeze(1).broadcast_to([P, KT, P]), ALU.mult,
                                  after=[c_ok, T.get(("fsumT", s - 1, i))])
                    st.dve(tt, nxt[:, 0, :], cur[:, 0, :], tw[:, 1, cols_], ALU.add, after=[w_ok])
                    ready_ = st.dve(tt, nxt[:, 1, :], cur[:, 1, :], tw[:, 0, cols_], ALU.subtract)
                    cur = nxt
                    yield
                T["cycles", s, i] = c_ok
                f_ok = st.dve(tt, f_sum[:, :, cols_], cur, x2T[:, :, cols_], ALU.add, after=[ready_])
                T["fsum", s, i] = f_ok
                yield
                for k in range(KT):
                    t = st.pe(tr, b.ap[:, k * P:(k + 1) * P], f_sum[:, k, cols_], ident[:, :], after=b.freed + [f_ok])
                T["fsumT", s, i] = t
                n_t, mean, rstd = norm_stats(st, "ffn", [b.ap[:, 0:D]], P, [t], first=i)
                stored = Token(s_out, 16 * s) if s else None
                t = st.dve(ts, out_sb[:, i, :], b.ap[:, 0:D], mean[0], rstd[0], ALU.subtract, ALU.mult,
                           after=[n_t, stored])
                b.freed = [t]
                T["out", s, i] = t
                yield

            gens = [chain(i, glob() if i == TT - 1 else iter(())) for i in range(TT)]
            for step in zip_longest(*gens[::-1]):
                pass
            ST.sp(nc.sync.dma_start, out[s].rearrange("(i p) d -> p i d", p=P), out_sb[:, :, :], by=16,
                  sem=Token(s_out, 16 * (s + 1)), after=[T["out", s, i] for i in range(TT)])

        c_cyc = sb("c_cyc", [P, 1])

        mixer_head(0)
        mixer_softplus(0)
        for p in range(NSEQ + 2):
            if p + 1 < NSEQ:
                load_seq(p + 1)
            if p < NSEQ:
                load_ctx(p)
            if p >= 2:
                ffn(p - 2)
            if p < NSEQ:
                mixer_prep(p)
                mixer_front(p)
            if 1 <= p <= NSEQ:
                attn_front(p - 1)
            if p < NSEQ:
                attn_context(p)
                mixer_back(p)
                attn_keys_in(p)
            if 1 <= p <= NSEQ:
                attn_back(p - 1)
            if p + 1 < NSEQ:
                mixer_head(p + 1)
                mixer_softplus(p + 1)
        queues = order(program)

        def play(name, engine):
            passed = {}
            for _, _, after, build, done, by, _, _ in queues[name]:
                need = {}
                for t in after:
                    if t.value > max(passed.get(id(t.sem), 0), need.get(id(t.sem), (0, None))[0]):
                        need[id(t.sem)] = (t.value, t.sem)
                for key, (value, sm) in need.items():
                    engine.wait_ge(sm, value)
                    passed[key] = value
                ins = build()
                if done is not None:
                    ins.then_inc(done.sem, by)

        block = es.enter_context(nc.Block())

        @block.tensor
        def _(e):
            play("pe", e)

        @block.scalar
        def _(e):
            play("act", e)

        @block.vector
        def _(e):
            play("dve", e)

        @block.gpsimd
        def _(e):
            play("pool", e)

        @block.sync
        def _(e):
            play("sp", e)
            e.wait_ge(s_out, 16 * NSEQ)


def kernel(**inputs):
    import numpy as np
    import concourse.bacc as bacc
    from concourse import mybir
    from concourse.bass_utils import run_bass_kernel_spmd as run

    a = {k: np.asarray(v) for k, v in inputs.items()}
    P, DI, NS, H, HD = 128, 512, 16, 8, 64
    f32 = np.float32
    x = np.ascontiguousarray(a["x"])

    w = a["L0_attn_W_in"]
    w_in = np.zeros((w.shape[1], 2 * DI + TAIL), f32)
    w_in[:, 0:DI] = w[DI:2 * DI].T
    w_in[:, DI:2 * DI] = w[0:DI].T
    w_in[:, 2 * DI + ROW_B:2 * DI + ROW_B + NS] = w[2 * DI:2 * DI + NS].T
    w_in[:, 2 * DI + ROW_C:2 * DI + ROW_C + NS] = w[2 * DI + NS:2 * DI + 2 * NS].T
    w_in[:, 2 * DI + ROW_DT:2 * DI + ROW_DT + H] = w[2 * DI + 2 * NS:].T

    cols, n = param_columns()
    par = np.zeros((P, n), f32)
    cw = a["L0_attn_conv_w"][:, 0, :]
    cb = a["L0_attn_conv_b"]
    for c in range(4):
        par[:, cols["conv_w"][0] + 4 * c:cols["conv_w"][0] + 4 * c + 4] = cw[c * P:(c + 1) * P]
        par[:, cols["conv_b"][0] + c] = cb[c * P:(c + 1) * P]
        par[0:HD, cols["D"][0] + c] = a["L0_attn_D"][2 * c]
        par[HD:P, cols["D"][0] + c] = a["L0_attn_D"][2 * c + 1]
        par[:, cols["norm_w"][0] + c] = a["L0_attn_norm_w"][c * P:(c + 1) * P]
    for row, at in ((ROW_B, DI), (ROW_C, DI + NS)):
        par[row:row + NS, cols["conv_w"][0] + 16:cols["conv_w"][0] + 20] = cw[at:at + NS]
        par[row:row + NS, cols["conv_b"][0] + 4] = cb[at:at + NS]
    for name, key in (("ln_m_w", "L0_xattn_ln_m_w"), ("ln_m_b", "L0_xattn_ln_m_b"), ("ln_l_w", "L0_xattn_ln_l_w"),
                      ("ln_l_b", "L0_xattn_ln_l_b"), ("cn_b1", "L0_ffn_cn_b1")):
        par[:, cols[name][0]:cols[name][1]] = a[key].reshape(2, P).T
    par[:, cols["cn_b2"][0]] = a["L0_ffn_cn_b2"]
    par[0:HD, cols["cn_b3"][0]] = a["L0_ffn_cn_b3"]
    par[:, cols["cn_b4"][0]] = a["L0_ffn_cn_b4"][0]
    par[:, cols["gc_b1"][0]] = a["L0_ffn_gc_b1"]
    par[0:HD, cols["gc_b2"][0]] = a["L0_ffn_gc_b2"]
    par[:, cols["gc_b3"][0]] = a["L0_ffn_gc_b3"][0]
    par[:, cols["range"][0]] = a["L0_ffn_adaptive_range"][0]
    par[ROW_DT:ROW_DT + H, cols["dt_bias"][0]] = a["L0_attn_dt_bias"]
    par[ROW_DT:ROW_DT + H, cols["A_log"][0]] = a["L0_attn_A_log"]

    arrays = {
        "x": x, "xT": np.ascontiguousarray(x.transpose(0, 2, 1)), "ctx": a["ctx_1024"], "par": par, "w_in": w_in,
        "w_out": a["L0_attn_W_out"].T, "wq": a["L0_xattn_Wq"], "wkv": a["L0_xattn_Wkv"], "wo": a["L0_xattn_Wout"],
        "cw1": a["L0_ffn_cn_w1"], "cw2": a["L0_ffn_cn_w2"], "cw3": a["L0_ffn_cn_w3"], "cw4": a["L0_ffn_cn_w4"],
        "gw1": a["L0_ffn_gc_w1"], "gw2": a["L0_ffn_gc_w2"], "gw3": a["L0_ffn_gc_w3"],
    }
    arrays = {k: np.ascontiguousarray(v) for k, v in arrays.items()}
    nc = bacc.Bacc("TRN2", target_bir_lowering=False, num_devices=1)
    dram = [nc.dram_tensor(f"in_{k}", v.shape, mybir.dt.float32, kind="ExternalInput").ap() for k, v in arrays.items()]
    result = nc.dram_tensor("result", x.shape, mybir.dt.float32, kind="ExternalOutput").ap()
    decoder_layer(nc, *dram, result)
    r = run(nc, [{f"in_{k}": v for k, v in arrays.items()}], core_ids=[0])
    return r.results[0]["result"]
```
